# Optimizing a Trainium2 kernel written in Bass

```python
import numpy as np
import jax
import jax.numpy as jnp

def _softmax(x, axis=-1):
    return jax.nn.softmax(x, axis=axis)

def _gelu(x):
    return jax.nn.gelu(x, approximate=True)

def _silu(x):
    return jax.nn.silu(x)

def _sigmoid(x):
    return jax.nn.sigmoid(x)

def _layernorm(x, axis=-1, eps=1e-05):
    m = jnp.mean(x, axis=axis, keepdims=True)
    v = jnp.var(x, axis=axis, keepdims=True)
    return (x - m) / jnp.sqrt(v + eps)

def _scatter_add(tgt, idx, src, axis=0):
    return tgt.at[idx].add(src)

def _segment_sum(src, seg, n):
    return jax.ops.segment_sum(src, seg, n)
kernel_name = 'mk_dlrm_tower_d1_rec_r8_8037b9'

def setup_inputs(seed: int=0):
    np.random.seed(seed)
    _w = jnp.asarray

    def _rec_inputs():
        import jax
        import jax.numpy as jnp
        _tk = jax.random.key(seed)
        dense_ctx = jax.random.normal(jax.random.fold_in(_tk, 190), (512, 16), jnp.float32)
        ids = jnp.stack([jax.random.randint(jax.random.fold_in(_tk, 200 + f), (512,), 0, v, jnp.int32) for f, v in enumerate([12500, 1000, 1250, 1250, 12500, 1000, 12500, 1250, 125000, 1250, 1250, 12500, 1250, 12500, 1250, 125000, 125000, 125000, 1250, 12500, 12500, 12500, 125000, 12500, 1000, 12500, 1250, 1000, 12500, 1250, 1250, 12500, 1250, 12500, 125000, 1000, 1250, 12500, 1250, 1250])], axis=1)
        tbl_0 = 0.05 * jax.random.normal(jax.random.fold_in(_tk, 500 + 0), (12500, 32), jnp.float32)
        tbl_1 = 0.05 * jax.random.normal(jax.random.fold_in(_tk, 500 + 1), (1000, 32), jnp.float32)
        tbl_2 = 0.05 * jax.random.normal(jax.random.fold_in(_tk, 500 + 2), (1250, 32), jnp.float32)
        tbl_3 = 0.05 * jax.random.normal(jax.random.fold_in(_tk, 500 + 3), (1250, 32), jnp.float32)
        tbl_4 = 0.05 * jax.random.normal(jax.random.fold_in(_tk, 500 + 4), (12500, 32), jnp.float32)
        tbl_5 = 0.05 * jax.random.normal(jax.random.fold_in(_tk, 500 + 5), (1000, 32), jnp.float32)
        tbl_6 = 0.05 * jax.random.normal(jax.random.fold_in(_tk, 500 + 6), (12500, 32), jnp.float32)
        tbl_7 = 0.05 * jax.random.normal(jax.random.fold_in(_tk, 500 + 7), (1250, 32), jnp.float32)
        tbl_8 = 0.05 * jax.random.normal(jax.random.fold_in(_tk, 500 + 8), (125000, 32), jnp.float32)
        tbl_9 = 0.05 * jax.random.normal(jax.random.fold_in(_tk, 500 + 9), (1250, 32), jnp.float32)
        tbl_10 = 0.05 * jax.random.normal(jax.random.fold_in(_tk, 500 + 10), (1250, 32), jnp.float32)
        tbl_11 = 0.05 * jax.random.normal(jax.random.fold_in(_tk, 500 + 11), (12500, 32), jnp.float32)
        tbl_12 = 0.05 * jax.random.normal(jax.random.fold_in(_tk, 500 + 12), (1250, 32), jnp.float32)
        tbl_13 = 0.05 * jax.random.normal(jax.random.fold_in(_tk, 500 + 13), (12500, 32), jnp.float32)
        tbl_14 = 0.05 * jax.random.normal(jax.random.fold_in(_tk, 500 + 14), (1250, 32), jnp.float32)
        tbl_15 = 0.05 * jax.random.normal(jax.random.fold_in(_tk, 500 + 15), (125000, 32), jnp.float32)
        tbl_16 = 0.05 * jax.random.normal(jax.random.fold_in(_tk, 500 + 16), (125000, 32), jnp.float32)
        tbl_17 = 0.05 * jax.random.normal(jax.random.fold_in(_tk, 500 + 17), (125000, 32), jnp.float32)
        tbl_18 = 0.05 * jax.random.normal(jax.random.fold_in(_tk, 500 + 18), (1250, 32), jnp.float32)
        tbl_19 = 0.05 * jax.random.normal(jax.random.fold_in(_tk, 500 + 19), (12500, 32), jnp.float32)
        tbl_20 = 0.05 * jax.random.normal(jax.random.fold_in(_tk, 500 + 20), (12500, 32), jnp.float32)
        tbl_21 = 0.05 * jax.random.normal(jax.random.fold_in(_tk, 500 + 21), (12500, 32), jnp.float32)
        tbl_22 = 0.05 * jax.random.normal(jax.random.fold_in(_tk, 500 + 22), (125000, 32), jnp.float32)
        tbl_23 = 0.05 * jax.random.normal(jax.random.fold_in(_tk, 500 + 23), (12500, 32), jnp.float32)
        tbl_24 = 0.05 * jax.random.normal(jax.random.fold_in(_tk, 500 + 24), (1000, 32), jnp.float32)
        tbl_25 = 0.05 * jax.random.normal(jax.random.fold_in(_tk, 500 + 25), (12500, 32), jnp.float32)
        tbl_26 = 0.05 * jax.random.normal(jax.random.fold_in(_tk, 500 + 26), (1250, 32), jnp.float32)
        tbl_27 = 0.05 * jax.random.normal(jax.random.fold_in(_tk, 500 + 27), (1000, 32), jnp.float32)
        tbl_28 = 0.05 * jax.random.normal(jax.random.fold_in(_tk, 500 + 28), (12500, 32), jnp.float32)
        tbl_29 = 0.05 * jax.random.normal(jax.random.fold_in(_tk, 500 + 29), (1250, 32), jnp.float32)
        tbl_30 = 0.05 * jax.random.normal(jax.random.fold_in(_tk, 500 + 30), (1250, 32), jnp.float32)
        tbl_31 = 0.05 * jax.random.normal(jax.random.fold_in(_tk, 500 + 31), (12500, 32), jnp.float32)
        tbl_32 = 0.05 * jax.random.normal(jax.random.fold_in(_tk, 500 + 32), (1250, 32), jnp.float32)
        tbl_33 = 0.05 * jax.random.normal(jax.random.fold_in(_tk, 500 + 33), (12500, 32), jnp.float32)
        tbl_34 = 0.05 * jax.random.normal(jax.random.fold_in(_tk, 500 + 34), (125000, 32), jnp.float32)
        tbl_35 = 0.05 * jax.random.normal(jax.random.fold_in(_tk, 500 + 35), (1000, 32), jnp.float32)
        tbl_36 = 0.05 * jax.random.normal(jax.random.fold_in(_tk, 500 + 36), (1250, 32), jnp.float32)
        tbl_37 = 0.05 * jax.random.normal(jax.random.fold_in(_tk, 500 + 37), (12500, 32), jnp.float32)
        tbl_38 = 0.05 * jax.random.normal(jax.random.fold_in(_tk, 500 + 38), (1250, 32), jnp.float32)
        tbl_39 = 0.05 * jax.random.normal(jax.random.fold_in(_tk, 500 + 39), (1250, 32), jnp.float32)
        _rk = jax.random.fold_in(_tk, 7)
        W_top1 = 0.049029 * jax.random.normal(jax.random.fold_in(_tk, 801), (416, 512), jnp.float32)
        W_top2 = 0.0441942 * jax.random.normal(jax.random.fold_in(_tk, 802), (512, 256), jnp.float32)
        W_top3 = 0.0625 * jax.random.normal(jax.random.fold_in(_tk, 803), (256, 1), jnp.float32)
        b_top1 = jnp.zeros((512,), jnp.float32)
        b_top2 = jnp.zeros((256,), jnp.float32)
        return (dense_ctx, ids, tbl_0, tbl_1, tbl_2, tbl_3, tbl_4, tbl_5, tbl_6, tbl_7, tbl_8, tbl_9, tbl_10, tbl_11, tbl_12, tbl_13, tbl_14, tbl_15, tbl_16, tbl_17, tbl_18, tbl_19, tbl_20, tbl_21, tbl_22, tbl_23, tbl_24, tbl_25, tbl_26, tbl_27, tbl_28, tbl_29, tbl_30, tbl_31, tbl_32, tbl_33, tbl_34, tbl_35, tbl_36, tbl_37, tbl_38, tbl_39, W_top1, b_top1, W_top2, b_top2, W_top3)
    dense_ctx, ids, tbl_0, tbl_1, tbl_2, tbl_3, tbl_4, tbl_5, tbl_6, tbl_7, tbl_8, tbl_9, tbl_10, tbl_11, tbl_12, tbl_13, tbl_14, tbl_15, tbl_16, tbl_17, tbl_18, tbl_19, tbl_20, tbl_21, tbl_22, tbl_23, tbl_24, tbl_25, tbl_26, tbl_27, tbl_28, tbl_29, tbl_30, tbl_31, tbl_32, tbl_33, tbl_34, tbl_35, tbl_36, tbl_37, tbl_38, tbl_39, W_top1, b_top1, W_top2, b_top2, W_top3 = _rec_inputs()

    def _L0_rec_setup():
        import jax, jax.numpy as jnp
        import numpy as np
        LAYER_SIZES = [200, 200, 200]
        key = jax.random.key(seed)
        ks = jax.random.split(key, 7)
        B, F, D = (256, 40, 32)
        field_nums = [F, 100, 100]
        inp = {'inputs': jax.random.normal(ks[0], (B, F, D), dtype=jnp.float32)}
        for i, size in enumerate(LAYER_SIZES):
            fan_in = field_nums[i] * F
            inp[f'W{i}'] = jax.random.normal(ks[1 + 2 * i], (size, fan_in), dtype=jnp.float32) * (1.0 / np.sqrt(fan_in))
            inp[f'b{i}'] = jnp.zeros((size,), dtype=jnp.float32)
        return inp
    _L0_rec_all = _L0_rec_setup()
    _L0_rec_in = {k: v for k, v in _L0_rec_all.items() if k in ('W0', 'b0', 'W1', 'b1', 'W2', 'b2')}
    del _L0_rec_all
    return {'dense_ctx': dense_ctx, 'ids': ids, 'tbl_0': tbl_0, 'tbl_1': tbl_1, 'tbl_2': tbl_2, 'tbl_3': tbl_3, 'tbl_4': tbl_4, 'tbl_5': tbl_5, 'tbl_6': tbl_6, 'tbl_7': tbl_7, 'tbl_8': tbl_8, 'tbl_9': tbl_9, 'tbl_10': tbl_10, 'tbl_11': tbl_11, 'tbl_12': tbl_12, 'tbl_13': tbl_13, 'tbl_14': tbl_14, 'tbl_15': tbl_15, 'tbl_16': tbl_16, 'tbl_17': tbl_17, 'tbl_18': tbl_18, 'tbl_19': tbl_19, 'tbl_20': tbl_20, 'tbl_21': tbl_21, 'tbl_22': tbl_22, 'tbl_23': tbl_23, 'tbl_24': tbl_24, 'tbl_25': tbl_25, 'tbl_26': tbl_26, 'tbl_27': tbl_27, 'tbl_28': tbl_28, 'tbl_29': tbl_29, 'tbl_30': tbl_30, 'tbl_31': tbl_31, 'tbl_32': tbl_32, 'tbl_33': tbl_33, 'tbl_34': tbl_34, 'tbl_35': tbl_35, 'tbl_36': tbl_36, 'tbl_37': tbl_37, 'tbl_38': tbl_38, 'tbl_39': tbl_39, 'W_top1': W_top1, 'b_top1': b_top1, 'W_top2': W_top2, 'b_top2': b_top2, 'W_top3': W_top3, 'L0_rec_W0': _L0_rec_in['W0'], 'L0_rec_b0': _L0_rec_in['b0'], 'L0_rec_W1': _L0_rec_in['W1'], 'L0_rec_b1': _L0_rec_in['b1'], 'L0_rec_W2': _L0_rec_in['W2'], 'L0_rec_b2': _L0_rec_in['b2']}

def reference(dense_ctx, ids, tbl_0, tbl_1, tbl_2, tbl_3, tbl_4, tbl_5, tbl_6, tbl_7, tbl_8, tbl_9, tbl_10, tbl_11, tbl_12, tbl_13, tbl_14, tbl_15, tbl_16, tbl_17, tbl_18, tbl_19, tbl_20, tbl_21, tbl_22, tbl_23, tbl_24, tbl_25, tbl_26, tbl_27, tbl_28, tbl_29, tbl_30, tbl_31, tbl_32, tbl_33, tbl_34, tbl_35, tbl_36, tbl_37, tbl_38, tbl_39, W_top1, b_top1, W_top2, b_top2, W_top3, L0_rec_W0, L0_rec_b0, L0_rec_W1, L0_rec_b1, L0_rec_W2, L0_rec_b2):
    import jax
    import jax.numpy as jnp

    def _L0_rec_ref(inputs, W0, b0, W1, b1, W2, b2):
        import jax, jax.numpy as jnp
        import numpy as np
        LAYER_SIZES = [200, 200, 200]
        params = [(W0, b0), (W1, b1), (W2, b2)]
        B, F, D = inputs.shape
        h = inputs
        outs = []
        n_layers = len(params)
        for i, (W, bias) in enumerate(params):
            x = jnp.einsum('bhd,bmd->bhmd', h, inputs).reshape(B, -1, D)
            y = jax.nn.relu(jnp.einsum('oi,bid->bod', W, x) + bias[None, :, None])
            if i != n_layers - 1:
                h, direct = jnp.split(y, 2, axis=1)
            else:
                direct = y
            outs.append(direct)
        result = jnp.concatenate(outs, axis=1)
        return result.sum(-1)
    e = jnp.stack([tbl_0[ids[:, 0]], tbl_1[ids[:, 1]], tbl_2[ids[:, 2]], tbl_3[ids[:, 3]], tbl_4[ids[:, 4]], tbl_5[ids[:, 5]], tbl_6[ids[:, 6]], tbl_7[ids[:, 7]], tbl_8[ids[:, 8]], tbl_9[ids[:, 9]], tbl_10[ids[:, 10]], tbl_11[ids[:, 11]], tbl_12[ids[:, 12]], tbl_13[ids[:, 13]], tbl_14[ids[:, 14]], tbl_15[ids[:, 15]], tbl_16[ids[:, 16]], tbl_17[ids[:, 17]], tbl_18[ids[:, 18]], tbl_19[ids[:, 19]], tbl_20[ids[:, 20]], tbl_21[ids[:, 21]], tbl_22[ids[:, 22]], tbl_23[ids[:, 23]], tbl_24[ids[:, 24]], tbl_25[ids[:, 25]], tbl_26[ids[:, 26]], tbl_27[ids[:, 27]], tbl_28[ids[:, 28]], tbl_29[ids[:, 29]], tbl_30[ids[:, 30]], tbl_31[ids[:, 31]], tbl_32[ids[:, 32]], tbl_33[ids[:, 33]], tbl_34[ids[:, 34]], tbl_35[ids[:, 35]], tbl_36[ids[:, 36]], tbl_37[ids[:, 37]], tbl_38[ids[:, 38]], tbl_39[ids[:, 39]]], axis=1)
    z = _L0_rec_ref(e, L0_rec_W0, L0_rec_b0, L0_rec_W1, L0_rec_b1, L0_rec_W2, L0_rec_b2)
    z = z.reshape(z.shape[0], -1)
    h = jnp.concatenate([z, dense_ctx], axis=1)
    h = jnp.maximum(h @ W_top1 + b_top1, 0.0)
    h = jnp.maximum(h @ W_top2 + b_top2, 0.0)
    y = h @ W_top3
    return y

_drawn_inputs = setup_inputs


def setup_inputs(seed=0):
    import zlib

    import numpy as np

    out = dict(_drawn_inputs(seed))
    spreads = {'b_top1': (0.0, 2.0),
     'b_top2': (0.0, 2.0),
     'L0_rec_b0': (0.0, 0.302),
     'L0_rec_b1': (0.0, 0.588),
     'L0_rec_b2': (0.0, 0.8)}
    factors = {'tbl_0': 8.0,
     'tbl_1': 8.0,
     'tbl_2': 8.0,
     'tbl_3': 8.0,
     'tbl_4': 8.0,
     'tbl_5': 8.0,
     'tbl_6': 8.0,
     'tbl_7': 8.0,
     'tbl_8': 8.0,
     'tbl_9': 8.0,
     'tbl_10': 8.0,
     'tbl_11': 8.0,
     'tbl_12': 8.0,
     'tbl_13': 8.0,
     'tbl_14': 8.0,
     'tbl_15': 8.0,
     'tbl_16': 8.0,
     'tbl_17': 8.0,
     'tbl_18': 8.0,
     'tbl_19': 8.0,
     'tbl_20': 8.0,
     'tbl_21': 8.0,
     'tbl_22': 8.0,
     'tbl_23': 8.0,
     'tbl_24': 8.0,
     'tbl_25': 8.0,
     'tbl_26': 8.0,
     'tbl_27': 8.0,
     'tbl_28': 8.0,
     'tbl_29': 8.0,
     'tbl_30': 8.0,
     'tbl_31': 8.0,
     'tbl_32': 8.0,
     'tbl_33': 8.0,
     'tbl_34': 8.0,
     'tbl_35': 8.0,
     'tbl_36': 8.0,
     'tbl_37': 8.0,
     'tbl_38': 8.0,
     'tbl_39': 8.0,
     'L0_rec_W0': 8.0,
     'L0_rec_W1': 8.0,
     'L0_rec_W2': 6.346,
     'dense_ctx': 8.0}
    for name, (base, spread) in spreads.items():
        noise = np.random.default_rng([zlib.crc32(name.encode()), seed]).standard_normal(out[name].shape)
        drawn = base * np.exp(spread * noise) if base else spread * noise
        out[name] = jnp.asarray(drawn.astype(out[name].dtype))
    for name, factor in factors.items():
        out[name] = (out[name] * factor).astype(out[name].dtype)
    return out
```

```python
from collections import namedtuple
from contextlib import ExitStack

import numpy as np

import concourse.bass as bass
from concourse import mybir

F32 = mybir.dt.float32
F32R = mybir.dt.float32r
I32 = mybir.dt.int32
ALU = mybir.AluOpType
ACT = mybir.ActivationFunctionType

FIELDS = 40
DIM = 32
LAYER = 200
HALF = LAYER // 2
DENSE = 16
TOP1, TOP2 = 512, 256

CHUNK = 128
COLS = 256
BLOCK = COLS // DIM
CG = COLS // 128
PER_CHUNK = CHUNK // BLOCK

SHIFTS = 3
TILES0 = (FIELDS // 2 + 1) // SHIFTS
PAIRS0 = SHIFTS * FIELDS
ROWS_X = FIELDS + SHIFTS * TILES0 - 1

HID_IN, FLD_IN = 25, 5
HID_OUT, FLD_OUT = HALF // HID_IN, FIELDS // FLD_IN
PAIRS = HID_IN * FLD_IN
TILES = HID_OUT * FLD_OUT
GROUP = 4
FLD_HALVES = FLD_OUT // GROUP
GROUPS = TILES // GROUP
GROUPS0 = 2
TILE_BASE = (0, TILES0, TILES0 + TILES)
ALL_TILES = TILES0 + 2 * TILES
OPERAND_ROWS = (PAIRS0 + 1, PAIRS + 1, PAIRS + 1)

PRODUCT_RING, SPLIT_RING = 3, 3
PREP_TILES = 5
Q_PARTS = 4

Place = namedtuple("Place", "group ring slot parity")


def cin_kernel(nc, ids, tables, w0a, w0b, w1, w2, dense_t, wt1z, wt1d, wt2, wt3, bt1, bt2,
               ident_in, sum32_in, out):
    batch = ids.shape[0]
    chunks = batch // CHUNK
    blocks = batch // BLOCK
    assert blocks % 2 == 0 and blocks >= 6
    last_groups = GROUPS0 + 2 * GROUPS

    def place(layer, block, odd=None):
        if odd is None:
            i = block + layer
            group = slot = 0
            for k in range(i):
                for lay, n in ((0, GROUPS0), (1, GROUPS), (2, GROUPS)):
                    if 0 <= k - lay < blocks:
                        group, slot = group + n, slot + 1
            for lay, n in ((0, GROUPS0), (1, GROUPS))[:layer]:
                if 0 <= i - lay < blocks:
                    group, slot = group + n, slot + 1
            return Place(group, group % 6, slot, slot % 2)
        at = place(layer, 4 + odd)
        return Place(block * last_groups + (at.group - (4 + odd) * last_groups), at.ring,
                     block * 3 + (at.slot - (4 + odd) * 3), at.parity)

    total_groups = blocks * last_groups
    total_slots = blocks * 3

    ctx = ExitStack()
    with ctx:
        def sb(name, shape, dt=F32):
            return ctx.enter_context(nc.sbuf_tensor(name, shape, dt))

        def ps(name, shape, dt=F32):
            return ctx.enter_context(nc.psum_tensor(name, shape, dt))

        def sem(name):
            return ctx.enter_context(nc.semaphore(name))

        x_rows = nc.dram_tensor("x_rows", [blocks, ROWS_X, COLS], F32, kind="Internal").ap()

        weights = sb("weights", [128, ALL_TILES, 2 * LAYER], F32R)
        x_pairs = sb("x_pairs", [128, 1 + TILES0, COLS])
        x_rep = sb("x_rep", [128, 2, FLD_OUT, COLS])
        hid_rep = [sb(f"hid_rep{n}", [128, HID_OUT, COLS]) for n in (1, 2)]
        product = sb("product", [128, PRODUCT_RING, GROUP, COLS])
        heads = sb("heads", [128, SPLIT_RING, GROUP, COLS], F32R)
        tails = sb("tails", [128, SPLIT_RING, GROUP, COLS], F32R)
        acc_copy = sb("acc_copy", [128, CG, 2 * LAYER])
        y_sum = sb("y_sum", [128, CG, LAYER])
        y_relu = sb("y_relu", [128, CG, LAYER])
        hid = [sb(f"hid{n}", [HALF, COLS]) for n in (1, 2)]
        z_t = sb("z_t", [HALF, Q_PARTS, batch])
        gathered = sb("gathered", [128, FIELDS, DIM])
        ids_all = sb("ids_all", [128, chunks, FIELDS], I32)
        ids_now = sb("ids_now", [128, FIELDS], I32)
        stored_flag = sb("stored_flag", [1, 2])
        ident = sb("ident", [128, 128])
        sum32 = sb("sum32", [128, 128 // DIM])
        dense_sb = sb("dense_sb", [DENSE, batch])
        wt1d_sb = sb("wt1d_sb", [DENSE, TOP1])
        wt3_sb = sb("wt3_sb", [128, TOP2 // 128])
        bt1_sb = sb("bt1_sb", [128, TOP1 // 128])
        bt2_sb = sb("bt2_sb", [128, TOP2 // 128])
        wt1z_sb = x_pairs[0:HALF, :, :].rearrange("p a c -> p (a c)").rearrange(
            "p (q n) -> p q n", q=Q_PARTS)
        wt2_sb = hid_rep[0][:, :, :]
        top1_act = product[:, :, :, :].rearrange("p a b c -> p (a b c)")[:, 0:TOP1 // 128 * batch].rearrange(
            "p (t n) -> p t n", t=TOP1 // 128)
        top2_act = hid_rep[1][:, :, :].rearrange("p a c -> p (a c)")[:, 0:TOP2 // 128 * batch].rearrange(
            "p (t n) -> p t n", t=TOP2 // 128)
        y_row = acc_copy[0:1, :, :].rearrange("p a c -> p (a c)")[:, 0:batch]

        acc = ps("acc", [128, 2, CG, 512])
        hid_ps = ps("hid_ps", [128, 2, 512])
        z_ps = ps("z_ps", [128, 2, 512])

        ids_loaded = sem("ids_loaded")
        consts_loaded = sem("consts_loaded")
        prep_loaded = [sem("prep_loaded0"), sem("prep_loaded1")]
        prep_added = sem("prep_added")
        weight_heads = sem("weight_heads")
        weight_tails = sem("weight_tails")
        ones_set = sem("ones_set")
        ids_copied = sem("ids_copied")
        x_gathered = sem("x_gathered")
        first_stored = sem("first_stored")
        x_stored = sem("x_stored")
        chunks_stored = sem("chunks_stored")
        pairs_loaded = sem("pairs_loaded")
        x_rep_loaded = [[sem(f"x_rep_loaded{p}{h}") for h in range(FLD_HALVES)] for p in range(2)]
        hid_loaded = [sem("hid_loaded1"), sem("hid_loaded2")]
        products_made = sem("products_made")
        heads_made = sem("heads_made")
        tails_made = sem("tails_made")
        groups_used = sem("groups_used")
        acc_copied = sem("acc_copied")
        y_summed = sem("y_summed")
        y_relued = sem("y_relued")
        y_turned = sem("y_turned")
        z_copied = sem("z_copied")
        hid_copied = [sem("hid_copied1"), sem("hid_copied2")]
        top_loaded = sem("top_loaded")
        top2_loaded = sem("top2_loaded")
        top1_done = sem("top1_done")
        top1_relued = sem("top1_relued")
        top2_done = sem("top2_done")
        top2_relued = sem("top2_relued")
        y_done = sem("y_done")
        y_copied = sem("y_copied")
        out_stored = sem("out_stored")

        PAIR_DMAS = 1 + SHIFTS
        STORED = 16 * 2 * PER_CHUNK
        prep = [(0, GROUP, True), (GROUP, TILES0 - GROUP, True)]
        for t in range(TILES0, ALL_TILES, PREP_TILES):
            prep.append((t, min(PREP_TILES, ALL_TILES - t), False))
        prep_uses = []
        uses = [0, 0]
        for n, (_, _, adds) in enumerate(prep):
            for half in ((0, 1) if adds else (n % 2,)):
                uses[half] += 1
            prep_uses.append(tuple(uses))

        def staging(half, n_tiles, rows):
            flat = product[0:rows, half, :, :].rearrange("p a c -> p (a c)")
            return flat[:, 0:n_tiles * LAYER].rearrange("p (t o) -> p t o", o=LAYER)

        def prep_rows(t):
            return OPERAND_ROWS[0] if t < TILES0 else OPERAND_ROWS[1]

        def above_zero(engine, semaphore, value):
            if not isinstance(value, int) or value > 0:
                engine.wait_ge(semaphore, value)

        def iterations(engine, step):
            for i in range(4):
                step(i, None)
            with engine.Fori(2, blocks // 2) as pair:
                step(pair * 2, 0)
                step(pair * 2 + 1, 1)
            step(blocks, None)
            step(blocks + 1, None)

        def where(layer, i, odd):
            if odd is None:
                return place(layer, i - layer) if 0 <= i - layer < blocks else None
            return place(layer, i - layer, (odd + layer) % 2)

        def loads_until(n, half):
            count = 0
            for m, (t, k, adds) in enumerate(prep[:n + 1]):
                if adds:
                    count += 1
                elif m % 2 == half:
                    count += sum(1 for layer in (1, 2)
                                 if max(t, TILE_BASE[layer]) < min(t + k, TILE_BASE[layer] + TILES))
            return count

        def group_tiles(layer, q):
            return TILES0 - GROUP if (layer, q) == (0, 1) else GROUP

        block = ctx.enter_context(nc.Block())

        @block.sync
        def _(sp):
            sp.dma_start(ids_all[:, :, :], ids.rearrange("(c p) f -> p c f", p=CHUNK)).then_inc(ids_loaded, 16)
            for dst, src in ((ident[:, :], ident_in), (sum32[:, :], sum32_in), (dense_sb[:, :], dense_t),
                             (wt1d_sb[:, :], wt1d), (wt3_sb[:, :], wt3), (bt1_sb[:, :], bt1), (bt2_sb[:, :], bt2)):
                sp.dma_start(dst, src).then_inc(consts_loaded, 16)
            for n, (t, k, adds) in enumerate(prep):
                if n > 0 and prep[n - 1][2]:
                    sp.wait_ge(weight_tails, n)
                elif n > 1:
                    sp.wait_ge(weight_tails, n - 1)
                if adds:
                    sp.dma_start(staging(0, k, prep_rows(t)), w0a[:, t:t + k, :]).then_inc(prep_loaded[0], 16)
                    sp.dma_start(staging(1, k, prep_rows(t)), w0b[:, t:t + k, :]).then_inc(prep_loaded[1], 16)
                else:
                    for layer, w in ((1, w1), (2, w2)):
                        first, end = max(t, TILE_BASE[layer]), min(t + k, TILE_BASE[layer] + TILES)
                        if first < end:
                            sp.dma_start(staging(n % 2, k, prep_rows(t))[:, first - t:end - t, :],
                                         w[:, first - TILE_BASE[layer]:end - TILE_BASE[layer], :]).then_inc(prep_loaded[n % 2], 16)
            sp.wait_ge(x_gathered, 16 * FIELDS)
            for b in range(PER_CHUNK):
                for field, rows in ((0, FIELDS), (FIELDS, ROWS_X - FIELDS)):
                    sp.dma_start(x_rows[b, field:field + rows, :].rearrange("m (s d) -> s m d", d=DIM),
                                 gathered[b * BLOCK:(b + 1) * BLOCK, 0:rows, :]).then_inc(first_stored, 16)
            sp.wait_ge(ones_set, 3)

            def load_pairs(b):
                sp.dma_start(x_pairs[0:PAIRS0, 0, :],
                             x_rows[b, 0:FIELDS, :].unsqueeze(0).to_broadcast([SHIFTS, FIELDS, COLS])).then_inc(pairs_loaded, 16)
                for j in range(SHIFTS):
                    rows = x_rows[b, j:j + FIELDS, :]
                    shifted = bass.AP(tensor=rows.tensor, offset=rows.offset,
                                      ap=[[COLS, FIELDS], [SHIFTS * COLS, TILES0], [1, COLS]])
                    sp.dma_start(x_pairs[j * FIELDS:(j + 1) * FIELDS, 1:1 + TILES0, :], shifted).then_inc(pairs_loaded, 16)

            def load_x_rep(b, parity, half):
                for g in range(half * GROUP, (half + 1) * GROUP):
                    fields = x_rows[b, g * FLD_IN:(g + 1) * FLD_IN, :]
                    sp.dma_start(x_rep[0:PAIRS, parity, g, :],
                                 fields.unsqueeze(0).to_broadcast([HID_IN, FLD_IN, COLS])).then_inc(x_rep_loaded[parity][half], 16)

            def load_hid(n):
                for g in range(HID_OUT):
                    maps = hid[n][g * HID_IN:(g + 1) * HID_IN, :]
                    sp.dma_start(hid_rep[n][0:PAIRS, g, :],
                                 maps.unsqueeze(1).to_broadcast([HID_IN, FLD_IN, COLS])).then_inc(hid_loaded[n], 16)

            def step(i, odd):
                l0, l1, l2 = (where(layer, i, odd) for layer in range(3))
                whole = odd is not None
                if whole or i + 1 < blocks:
                    sp.wait_ge(products_made, l0.group + GROUPS0)
                    sp.wait_ge(chunks_stored, (i + 1) // PER_CHUNK + 1)
                    load_pairs(i + 1)
                if whole or i < blocks:
                    if l1 is not None:
                        sp.wait_ge(products_made, l1.group + GROUPS)
                    sp.wait_ge(hid_copied[0], i + 1)
                    load_hid(0)
                    parity = i % 2 if odd is None else odd
                    for half in range(FLD_HALVES):
                        if l2 is not None:
                            sp.wait_ge(products_made, l2.group + (half + 1) * HID_OUT)
                        load_x_rep(i, parity, half)
                if l1 is not None:
                    if l2 is not None:
                        sp.wait_ge(products_made, l2.group + GROUPS)
                    sp.wait_ge(hid_copied[1], i)
                    load_hid(1)

            sp.wait_ge(first_stored, STORED)
            load_pairs(0)
            for i in range(4):
                step(i, None)
            with sp.Fori(2, blocks // 2 - 1) as pair:
                step(pair * 2, 0)
                step(pair * 2 + 1, 1)
            step(blocks - 2, None)
            step(blocks - 1, None)
            sp.wait_ge(products_made, place(0, blocks - 1).group + GROUPS0)
            sp.dma_start(wt1z_sb, wt1z).then_inc(top_loaded, 16)
            step(blocks, None)
            sp.wait_ge(products_made, place(1, blocks - 1).group + GROUPS)
            sp.dma_start(wt2_sb, wt2).then_inc(top2_loaded, 16)
            sp.wait_ge(y_copied, 1)
            sp.dma_start(out.rearrange("b o -> o b"), y_row).then_inc(out_stored, 16)
            sp.wait_ge(out_stored, 16)

        @block.gpsimd
        def _(pool):
            def gather(f, ids_of_field):
                pool.indirect_dma_start(gathered[:, f, :], None, tables[f],
                                        bass.IndirectOffsetOnAxis(ids_of_field, 0)).then_inc(x_gathered, 16)

            def add(s):
                pool.wait_ge(acc_copied, s + 1)
                above_zero(pool, y_relued, s)
                pool.tensor_tensor(y_sum[:, :, :], acc_copy[:, :, 0:LAYER], acc_copy[:, :, LAYER:2 * LAYER],
                                   ALU.add).then_inc(y_summed, 1)

            pool.wait_ge(ids_loaded, 16)
            for f in range(FIELDS):
                gather(f, ids_all[:, 0, f:f + 1])
            pool.wait_ge(first_stored, STORED)
            pool.memset(stored_flag[:, :], 0.0).then_inc(chunks_stored, 1)
            adds = FIELDS // 2 + PER_CHUNK
            done = 1 + (chunks - 1) * adds
            add(0)
            if chunks > 1:
                with pool.Fori(1, chunks) as c:
                    first = 1 + (c - 1) * adds
                    pool.tensor_copy(ids_now[:, :], ids_all[:, bass.ds(c, 1), :].rearrange("p c f -> p (c f)")).then_inc(ids_copied, 1)
                    pool.wait_ge(ids_copied, c)
                    for k in range(FIELDS // 2):
                        add(first + k)
                        gather(2 * k, ids_now[:, 2 * k:2 * k + 1])
                        gather(2 * k + 1, ids_now[:, 2 * k + 1:2 * k + 2])
                    pool.wait_ge(x_gathered, (c + 1) * (16 * FIELDS))
                    for b in range(PER_CHUNK):
                        add(first + FIELDS // 2 + b)
                        for field, rows in ((0, FIELDS), (FIELDS, ROWS_X - FIELDS)):
                            pool.dma_start(x_rows[c * PER_CHUNK + b, field:field + rows, :].rearrange("m (s d) -> s m d", d=DIM),
                                           gathered[b * BLOCK:(b + 1) * BLOCK, 0:rows, :]).then_inc(x_stored, 16)
                    pool.wait_ge(x_stored, c * STORED)
                    pool.tensor_tensor(stored_flag[:, 1:2], stored_flag[:, 0:1], stored_flag[:, 0:1], ALU.add).then_inc(chunks_stored, 1)
            with pool.Fori(done, total_slots) as s:
                add(s)

        @block.scalar
        def _(act):
            for n, (t, k, adds) in enumerate(prep):
                rows = prep_rows(t)
                if adds:
                    act.wait_ge(prep_added, n + 1)
                else:
                    act.wait_ge(prep_loaded[n % 2], 16 * loads_until(n, n % 2))
                act.activation(weights[0:rows, t:t + k, 0:LAYER],
                               staging(0 if adds else n % 2, k, rows), ACT.Copy).then_inc(weight_heads, 1)

            def make_heads(layer, at, q):
                g, ring = at.group + q, (at.ring + q) % 6
                tiles = group_tiles(layer, q)
                act.wait_ge(products_made, g + 1)
                above_zero(act, groups_used, g - (SPLIT_RING - 1))
                rows = OPERAND_ROWS[layer]
                act.activation(heads[0:rows, ring % SPLIT_RING, 0:tiles, :], product[0:rows, ring % PRODUCT_RING, 0:tiles, :],
                               ACT.Copy).then_inc(heads_made, 1)

            def copy_acc(layer, at):
                act.wait_ge(groups_used, at.group + (GROUPS, GROUPS0)[layer == 0])
                above_zero(act, y_summed, at.slot)
                act.activation(acc_copy[:, :, :], acc[:, at.parity, :, 0:2 * LAYER], ACT.Copy).then_inc(acc_copied, 1)

            def relu(at):
                act.wait_ge(y_summed, at.slot + 1)
                above_zero(act, y_turned, at.slot)
                act.activation(y_relu[:, :, :], y_sum[:, :, :], ACT.Relu).then_inc(y_relued, 1)

            def copy_turned(layer, at, b):
                act.wait_ge(y_turned, at.slot + 1)
                cols = slice(b * BLOCK, (b + 1) * BLOCK) if isinstance(b, int) else bass.ds(b * BLOCK, BLOCK)
                if layer < 2:
                    above_zero(act, hid_loaded[layer], b * (16 * HID_OUT))
                    act.activation(hid[layer][:, :], hid_ps[0:HALF, layer, 0:COLS], ACT.Copy).then_inc(hid_copied[layer], 1)
                    act.activation(z_t[:, layer, cols], z_ps[0:HALF, at.parity, 0:BLOCK], ACT.Copy).then_inc(z_copied, 1)
                else:
                    act.activation(z_t[:, 2:4, cols],
                                   z_ps[0:HALF, at.parity, 0:2 * BLOCK].rearrange("p (q b) -> p q b", q=2),
                                   ACT.Copy).then_inc(z_copied, 1)

            def step(i, odd):
                l0, l1, l2 = (where(layer, i, odd) for layer in range(3))
                if odd is None:
                    before = place(2, i - 3) if 0 <= i - 3 < blocks else None
                else:
                    before = Place(l0.group - GROUPS, (l0.ring - GROUPS) % 6, l0.slot - 1, (l0.parity + 1) % 2)
                if l0:
                    make_heads(0, l0, 0)
                    make_heads(0, l0, 1)
                if before:
                    copy_acc(2, before)
                if l1:
                    make_heads(1, l1, 0)
                if before:
                    relu(before)
                if l1:
                    make_heads(1, l1, 1)
                if l0:
                    copy_acc(0, l0)
                if l1:
                    make_heads(1, l1, 2)
                if before:
                    copy_turned(2, before, i - 3)
                if l0:
                    relu(l0)
                if l1:
                    make_heads(1, l1, 3)
                    make_heads(1, l1, 4)
                if l0:
                    copy_turned(0, l0, i)
                if l1:
                    for q in range(5, GROUPS):
                        make_heads(1, l1, q)
                if l2:
                    make_heads(2, l2, 0)
                    make_heads(2, l2, 1)
                if l1:
                    copy_acc(1, l1)
                if l2:
                    make_heads(2, l2, 2)
                if l1:
                    relu(l1)
                if l2:
                    make_heads(2, l2, 3)
                    make_heads(2, l2, 4)
                if l1:
                    copy_turned(1, l1, i - 1)
                if l2:
                    for q in range(5, GROUPS):
                        make_heads(2, l2, q)

            iterations(act, step)
            step(blocks + 2, None)

            act.wait_ge(consts_loaded, 16 * 7)
            act.wait_ge(tails_made, total_groups)
            for t in range(TOP1 // 128):
                act.wait_ge(top1_done, t + 1)
                act.activation(top1_act[:, t, :], acc[:, t // CG, t % CG, 0:batch], ACT.Relu,
                               bias=bt1_sb[:, t:t + 1]).then_inc(top1_relued, 1)
            for t in range(TOP2 // 128):
                act.wait_ge(top2_done, t + 1)
                act.activation(top2_act[:, t, :], hid_ps[:, t, 0:batch], ACT.Relu,
                               bias=bt2_sb[:, t:t + 1]).then_inc(top2_relued, 1)
            act.wait_ge(y_done, 1)
            act.activation(y_row, z_ps[0:1, 0, 0:batch], ACT.Copy).then_inc(y_copied, 1)

        @block.vector
        def _(dve):
            dve.memset(x_pairs[:, :, :], 1.0).then_inc(ones_set, 1)
            dve.memset(x_rep[:, :, :, :], 1.0).then_inc(ones_set, 1)
            dve.memset(hid_rep[0][:, :, :], 1.0)
            dve.memset(hid_rep[1][:, :, :], 1.0).then_inc(ones_set, 1)
            for n, (t, k, adds) in enumerate(prep):
                rows = prep_rows(t)
                raw = staging(0 if adds else n % 2, k, rows)
                if adds:
                    dve.wait_ge(prep_loaded[0], 16 * (n + 1))
                    dve.wait_ge(prep_loaded[1], 16 * (n + 1))
                    dve.tensor_tensor(raw, raw, staging(1, k, rows), ALU.add).then_inc(prep_added, 1)
                dve.wait_ge(weight_heads, n + 1)
                dve.tensor_tensor(weights[0:rows, t:t + k, LAYER:2 * LAYER], raw,
                                  weights[0:rows, t:t + k, 0:LAYER].bitcast(F32), ALU.subtract).then_inc(weight_tails, 1)

            def make_product(layer, at, q, b, parity):
                g, ring = at.group + q, (at.ring + q) % 6
                tiles, rows = group_tiles(layer, q), OPERAND_ROWS[layer]
                if layer == 0:
                    if q == 0:
                        dve.wait_ge(pairs_loaded, (b + 1) * (16 * PAIR_DMAS))
                    first, second = x_pairs[0:rows, 0, :], x_pairs[0:rows, 1 + GROUP * q:1 + GROUP * q + tiles, :]
                else:
                    half, hid_block = q // HID_OUT, q % HID_OUT
                    if q == 0:
                        dve.wait_ge(hid_loaded[layer - 1], (b + 1) * (16 * HID_OUT))
                    if hid_block == 0 and layer == 1:
                        if isinstance(b, int):
                            dve.wait_ge(x_rep_loaded[parity][half], (b // 2 + 1) * (16 * GROUP))
                        else:
                            dve.wait_ge(x_rep_loaded[parity][half], (b - parity + 2) * (8 * GROUP))
                    first = hid_rep[layer - 1][0:rows, hid_block, :]
                    second = x_rep[0:rows, parity, half * GROUP:(half + 1) * GROUP, :]
                above_zero(dve, tails_made, g - (PRODUCT_RING - 1))
                dve.tensor_tensor(product[0:rows, ring % PRODUCT_RING, 0:tiles, :],
                                  first.unsqueeze(1).to_broadcast([rows, tiles, COLS]), second,
                                  ALU.mult).then_inc(products_made, 1)

            def make_tails(layer, q, g, ring):
                tiles, rows = group_tiles(layer, q), OPERAND_ROWS[layer]
                dve.wait_ge(heads_made, g + 1)
                above_zero(dve, groups_used, g - (SPLIT_RING - 1))
                dve.tensor_tensor(tails[0:rows, ring % SPLIT_RING, 0:tiles, :],
                                  product[0:rows, ring % PRODUCT_RING, 0:tiles, :],
                                  heads[0:rows, ring % SPLIT_RING, 0:tiles, :].bitcast(F32),
                                  ALU.subtract).then_inc(tails_made, 1)

            previous = [None]

            def step(i, odd):
                for layer in range(3):
                    at = where(layer, i, odd)
                    if at is None:
                        continue
                    parity = (i - layer) % 2 if odd is None else (odd + layer) % 2
                    for q in range((GROUPS, GROUPS0)[layer == 0]):
                        make_product(layer, at, q, i - layer, parity)
                        if previous[0]:
                            make_tails(*previous[0], at.group + q - 1, (at.ring + q - 1) % 6)
                        previous[0] = (layer, q)

            dve.wait_ge(ones_set, 3)
            dve.wait_ge(weight_tails, len(prep))
            iterations(dve, step)
            make_tails(*previous[0], total_groups - 1, (total_groups - 1) % 6)

        @block.tensor
        def _(pe):
            pe.wait_ge(weight_tails, len(prep))
            pe.wait_ge(consts_loaded, 16 * 7)

            def accumulate(layer, at, q):
                g, ring = at.group + q, (at.ring + q) % 6
                rows, last_q = OPERAND_ROWS[layer], (GROUPS, GROUPS0)[layer == 0] - 1
                if q == 0:
                    above_zero(pe, acc_copied, at.slot - 1)
                pe.wait_ge(tails_made, g + 1)
                tiles = group_tiles(layer, q)
                for k in range(tiles):
                    w = weights[0:rows, TILE_BASE[layer] + GROUP * q + k, :]
                    for c in range(CG):
                        cols = slice(c * 128, (c + 1) * 128)
                        nc.tensor.matmul(acc[:, at.parity, c, 0:2 * LAYER], heads[0:rows, ring % SPLIT_RING, k, cols], w,
                                         start=(q == 0 and k == 0), stop=False)
                        last = nc.tensor.matmul(acc[:, at.parity, c, LAYER:2 * LAYER], tails[0:rows, ring % SPLIT_RING, k, cols],
                                                w[:, 0:LAYER], start=False, stop=(q == last_q and k == tiles - 1))
                last.then_inc(groups_used, 1)

            def turn(layer, at, b):
                pe.wait_ge(y_relued, at.slot + 1)
                above_zero(pe, z_copied, at.slot - 1)
                if layer < 2:
                    above_zero(pe, hid_copied[layer], b)
                    for c in range(CG):
                        nc.tensor.transpose(hid_ps[0:HALF, layer, c * 128:(c + 1) * 128], y_relu[:, c, 0:HALF], ident[:, :])
                for n, first in enumerate((HALF,) if layer < 2 else (0, HALF)):
                    for c in range(CG):
                        at_col = n * BLOCK + c * (BLOCK // CG)
                        last = nc.tensor.matmul(z_ps[0:HALF, at.parity, at_col:at_col + BLOCK // CG],
                                                y_relu[:, c, first:first + HALF], sum32[:, :], start=True, stop=True)
                last.then_inc(y_turned, 1)

            def step(i, odd):
                l0, l1, l2 = (where(layer, i, odd) for layer in range(3))
                if odd is None:
                    before = place(2, i - 3) if 0 <= i - 3 < blocks else None
                else:
                    before = Place(l0.group - GROUPS, (l0.ring - GROUPS) % 6, l0.slot - 1, (l0.parity + 1) % 2)
                if l0:
                    for q in range(GROUPS0):
                        accumulate(0, l0, q)
                if before:
                    turn(2, before, i - 3)
                for q in range(GROUPS):
                    if l1:
                        accumulate(1, l1, q)
                    if q == 1 and l0:
                        turn(0, l0, i)
                for q in range(GROUPS):
                    if l2:
                        accumulate(2, l2, q)
                    if q == 1 and l1:
                        turn(1, l1, i - 1)

            iterations(pe, step)
            step(blocks + 2, None)

            pe.wait_ge(z_copied, total_slots)
            pe.wait_ge(top_loaded, 16)
            for t in range(TOP1 // 128):
                cols = slice(t * 128, (t + 1) * 128)
                for q in range(Q_PARTS):
                    nc.tensor.matmul(acc[:, t // CG, t % CG, 0:batch], wt1z_sb[:, q, cols], z_t[:, q, :],
                                     start=(q == 0), stop=False)
                nc.tensor.matmul(acc[:, t // CG, t % CG, 0:batch], wt1d_sb[:, cols], dense_sb[:, :],
                                 start=False, stop=True).then_inc(top1_done, 1)
            pe.wait_ge(top2_loaded, 16)
            for k in range(TOP1 // 128):
                pe.wait_ge(top1_relued, k + 1)
                for t in range(TOP2 // 128):
                    last = nc.tensor.matmul(hid_ps[:, t, 0:batch], wt2_sb[:, k, t * 128:(t + 1) * 128], top1_act[:, k, :],
                                            start=(k == 0), stop=(k == TOP1 // 128 - 1))
                    if k == TOP1 // 128 - 1:
                        last.then_inc(top2_done, 1)
            for k in range(TOP2 // 128):
                pe.wait_ge(top2_relued, k + 1)
                last = nc.tensor.matmul(z_ps[0:1, 0, 0:batch], wt3_sb[:, k:k + 1], top2_act[:, k, :],
                                        start=(k == 0), stop=(k == TOP2 // 128 - 1))
            last.then_inc(y_done, 1)


def lay_out(inputs):
    def arr(name):
        return np.asarray(inputs[name])

    shift = np.arange(SHIFTS)[:, None, None] + SHIFTS * np.arange(TILES0)[None, None, :]
    i = np.arange(FIELDS)[None, :, None]
    i, m = np.broadcast_arrays(i, (i + shift) % FIELDS)
    w = arr("L0_rec_W0").reshape(LAYER, FIELDS, FIELDS)
    w0a = np.zeros((PAIRS0 + 1, TILES0, LAYER), w.dtype)
    w0b = np.zeros((PAIRS0 + 1, TILES0, LAYER), w.dtype)
    w0a[:PAIRS0] = w[:, i, m].transpose(1, 2, 3, 0).reshape(PAIRS0, TILES0, LAYER)
    w0a[PAIRS0, 0] = arr("L0_rec_b0")
    w0b[:PAIRS0] = w[:, m, i].transpose(1, 2, 3, 0).reshape(PAIRS0, TILES0, LAYER)
    w0b[0:FIELDS, 0] = 0
    w0b[PAIRS0 - FIELDS:PAIRS0, TILES0 - 1] = 0
    packed = {"ids": arr("ids"), "w0a": w0a, "w0b": w0b}
    for n in (1, 2):
        w = arr(f"L0_rec_W{n}").reshape(LAYER, HID_OUT, HID_IN, FLD_HALVES, GROUP, FLD_IN)
        full = np.zeros((PAIRS + 1, TILES, LAYER), w.dtype)
        full[:PAIRS] = w.transpose(2, 5, 3, 1, 4, 0).reshape(PAIRS, TILES, LAYER)
        full[PAIRS, 0] = arr(f"L0_rec_b{n}")
        packed[f"w{n}"] = full
    wt1 = arr("W_top1")
    packed["dense_t"] = np.ascontiguousarray(arr("dense_ctx").T)
    packed["wt1z"] = np.ascontiguousarray(wt1[:2 * LAYER].reshape(Q_PARTS, HALF, TOP1).transpose(1, 0, 2))
    packed["wt1d"] = np.ascontiguousarray(wt1[2 * LAYER:])
    packed["wt2"] = np.ascontiguousarray(arr("W_top2").reshape(TOP1 // 128, 128, TOP2).transpose(1, 0, 2))
    packed["wt3"] = np.ascontiguousarray(arr("W_top3").reshape(TOP2 // 128, 128).T)
    packed["bt1"] = np.ascontiguousarray(arr("b_top1").reshape(TOP1 // 128, 128).T)
    packed["bt2"] = np.ascontiguousarray(arr("b_top2").reshape(TOP2 // 128, 128).T)
    packed["ident"] = np.eye(128, dtype=np.float32)
    packed["sum32"] = np.repeat(np.eye(128 // DIM, dtype=np.float32), DIM, axis=0)
    for f in range(FIELDS):
        packed[f"tbl_{f}"] = arr(f"tbl_{f}")
    return packed


def build(nc, packed, batch):
    def dram(name):
        a = packed[name]
        return nc.dram_tensor(f"in_{name}", a.shape, mybir.dt.from_np(a.dtype), kind="ExternalInput").ap()

    args = {name: dram(name) for name in packed}
    out = nc.dram_tensor("out_y", (batch, 1), F32, kind="ExternalOutput").ap()
    cin_kernel(nc, args["ids"], [args[f"tbl_{f}"] for f in range(FIELDS)], args["w0a"], args["w0b"], args["w1"],
               args["w2"], args["dense_t"], args["wt1z"], args["wt1d"], args["wt2"], args["wt3"], args["bt1"],
               args["bt2"], args["ident"], args["sum32"], out)


def kernel(**inputs):
    import concourse.bacc as bacc
    from concourse.bass_utils import run_bass_kernel_spmd

    packed = lay_out(inputs)
    nc = bacc.Bacc("TRN2", target_bir_lowering=False, num_devices=1)
    build(nc, packed, packed["ids"].shape[0])
    r = run_bass_kernel_spmd(nc, [{f"in_{name}": a for name, a in packed.items()}], core_ids=[0])
    return r.results[0]["out_y"]
```

```python
from collections import namedtuple
from contextlib import ExitStack

import numpy as np

import concourse.bass as bass
from concourse import mybir

F32 = mybir.dt.float32
F32R = mybir.dt.float32r
I32 = mybir.dt.int32
ALU = mybir.AluOpType
ACT = mybir.ActivationFunctionType

FIELDS = 40
DIM = 32
LAYER = 200
HALF = LAYER // 2
DENSE = 16
TOP1, TOP2 = 512, 256

CHUNK = 128
COLS = 256
BLOCK = COLS // DIM
CG = COLS // 128
PER_CHUNK = CHUNK // BLOCK

SHIFTS = 3
TILES0 = (FIELDS // 2 + 1) // SHIFTS
PAIRS0 = SHIFTS * FIELDS
ROWS_X = FIELDS + SHIFTS * TILES0 - 1

HID_IN, FLD_IN = 25, 5
HID_OUT, FLD_OUT = HALF // HID_IN, FIELDS // FLD_IN
PAIRS = HID_IN * FLD_IN
TILES = HID_OUT * FLD_OUT
GROUP = 4
FLD_HALVES = FLD_OUT // GROUP
GROUPS = TILES // GROUP
GROUPS0 = 2
TILE_BASE = (0, TILES0, TILES0 + TILES)
ALL_TILES = TILES0 + 2 * TILES
OPERAND_ROWS = (PAIRS0 + 1, PAIRS + 1, PAIRS + 1)

PRODUCT_RING, SPLIT_RING = 3, 3
PREP_TILES = 5
Q_PARTS = 4

Place = namedtuple("Place", "group ring slot parity")


def cin_kernel(nc, ids, tables, w0a, w0b, w1, w2, dense_t, wt1z, wt1d, wt2, wt3, bt1, bt2,
               ident_in, sum32_in, out):
    batch = ids.shape[0]
    chunks = batch // CHUNK
    blocks = batch // BLOCK
    assert blocks % 2 == 0 and blocks >= 6
    last_groups = GROUPS0 + 2 * GROUPS

    def place(layer, block, odd=None):
        if odd is None:
            i = block + layer
            group = slot = 0
            for k in range(i):
                for lay, n in ((0, GROUPS0), (1, GROUPS), (2, GROUPS)):
                    if 0 <= k - lay < blocks:
                        group, slot = group + n, slot + 1
            for lay, n in ((0, GROUPS0), (1, GROUPS))[:layer]:
                if 0 <= i - lay < blocks:
                    group, slot = group + n, slot + 1
            return Place(group, group % 6, slot, slot % 2)
        at = place(layer, 4 + odd)
        return Place(block * last_groups + (at.group - (4 + odd) * last_groups), at.ring,
                     block * 3 + (at.slot - (4 + odd) * 3), at.parity)

    total_groups = blocks * last_groups
    total_slots = blocks * 3

    ctx = ExitStack()
    with ctx:
        def sb(name, shape, dt=F32):
            return ctx.enter_context(nc.sbuf_tensor(name, shape, dt))

        def ps(name, shape, dt=F32):
            return ctx.enter_context(nc.psum_tensor(name, shape, dt))

        def sem(name):
            return ctx.enter_context(nc.semaphore(name))

        x_rows = nc.dram_tensor("x_rows", [blocks, ROWS_X, COLS], F32, kind="Internal").ap()

        weights = sb("weights", [128, ALL_TILES, 2 * LAYER], F32R)
        x_pairs = sb("x_pairs", [128, 1 + TILES0, COLS])
        x_rep = sb("x_rep", [128, 2, FLD_OUT, COLS])
        hid_rep = [sb(f"hid_rep{n}", [128, HID_OUT, COLS]) for n in (1, 2)]
        product = sb("product", [128, PRODUCT_RING, GROUP, COLS])
        heads = sb("heads", [128, SPLIT_RING, GROUP, COLS], F32R)
        tails = sb("tails", [128, SPLIT_RING, GROUP, COLS], F32R)
        acc_copy = sb("acc_copy", [128, CG, 2 * LAYER])
        y_relu = sb("y_relu", [128, CG, LAYER])
        hid = [sb(f"hid{n}", [HALF, COLS]) for n in (1, 2)]
        z_t = sb("z_t", [HALF, Q_PARTS, batch])
        gathered = sb("gathered", [128, FIELDS, DIM])
        ids_all = sb("ids_all", [128, chunks, FIELDS], I32)
        ids_now = sb("ids_now", [128, FIELDS], I32)
        wait_taker = sb("wait_taker", [1, 3])
        ident = sb("ident", [128, 128])
        sum32 = sb("sum32", [128, 128 // DIM])
        dense_sb = sb("dense_sb", [DENSE, batch])
        wt1d_sb = sb("wt1d_sb", [DENSE, TOP1])
        wt3_sb = sb("wt3_sb", [128, TOP2 // 128])
        bt1_sb = sb("bt1_sb", [128, TOP1 // 128])
        bt2_sb = sb("bt2_sb", [128, TOP2 // 128])
        wt1z_sb = x_pairs[0:HALF, :, :].rearrange("p a c -> p (a c)").rearrange(
            "p (q n) -> p q n", q=Q_PARTS)
        wt2_sb = hid_rep[0][:, :, :]
        top1_act = product[:, :, :, :].rearrange("p a b c -> p (a b c)")[:, 0:TOP1 // 128 * batch].rearrange(
            "p (t n) -> p t n", t=TOP1 // 128)
        top2_act = hid_rep[1][:, :, :].rearrange("p a c -> p (a c)")[:, 0:TOP2 // 128 * batch].rearrange(
            "p (t n) -> p t n", t=TOP2 // 128)
        y_row = acc_copy[0:1, :, :].rearrange("p a c -> p (a c)")[:, 0:batch]

        acc = ps("acc", [128, 2, CG, 512])
        hid_ps = ps("hid_ps", [128, 2, 512])
        z_ps = ps("z_ps", [128, 2, 512])

        ids_loaded = sem("ids_loaded")
        consts_loaded = sem("consts_loaded")
        prep_loaded = [sem(f"prep_loaded{n}") for n in range(PRODUCT_RING)]
        swapped_loaded = [sem(f"swapped_loaded{n}") for n in range(2)]
        prep_added = sem("prep_added")
        weight_heads = sem("weight_heads")
        weight_tails = sem("weight_tails")
        ones_set = sem("ones_set")
        ids_copied = sem("ids_copied")
        taker_set = sem("taker_set")
        waits_taken = sem("waits_taken")
        x_gathered = sem("x_gathered")
        early_gathered = sem("early_gathered")
        early_stored = sem("early_stored")
        block0_stored = sem("block0_stored")
        first_stored = sem("first_stored")
        x_stored = sem("x_stored")
        chunks_stored = sem("chunks_stored")
        pairs_loaded = sem("pairs_loaded")
        x_rep_loaded = [[sem(f"x_rep_loaded{p}{h}") for h in range(FLD_HALVES)] for p in range(2)]
        hid_loaded = [sem("hid_loaded1"), sem("hid_loaded2")]
        products_made = sem("products_made")
        heads_made = sem("heads_made")
        tails_made = sem("tails_made")
        groups_used = sem("groups_used")
        acc_copied = sem("acc_copied")
        y_summed = sem("y_summed")
        y_relued = sem("y_relued")
        y_turned = sem("y_turned")
        z_copied = sem("z_copied")
        hid_copied = [sem("hid_copied1"), sem("hid_copied2")]
        top_loaded = sem("top_loaded")
        top2_loaded = sem("top2_loaded")
        top1_done = sem("top1_done")
        top1_relued = sem("top1_relued")
        top2_done = sem("top2_done")
        top2_relued = sem("top2_relued")
        y_done = sem("y_done")
        y_copied = sem("y_copied")
        out_stored = sem("out_stored")

        PAIR_DMAS = 1 + SHIFTS
        STORED = 16 * 2 * PER_CHUNK
        prep = [(0, GROUP, w0a[:, 0:GROUP, :]), (GROUP, TILES0 - GROUP, w0a[:, GROUP:TILES0, :])]
        for layer, w in ((1, w1), (2, w2)):
            for t in range(0, TILES, PREP_TILES):
                k = min(PREP_TILES, TILES - t)
                prep.append((TILE_BASE[layer] + t, k, w[:, t:t + k, :]))
        split_until = [2, 2 + -(-TILES // PREP_TILES), len(prep)]

        def staging(n):
            t, k, _ = prep[n]
            flat = product[0:prep_rows(t), n % PRODUCT_RING, :, :].rearrange("p a c -> p (a c)")
            return flat[:, 0:k * LAYER].rearrange("p (t o) -> p t o", o=LAYER)

        def swapped(n):
            t, k, _ = prep[n]
            flat = hid_rep[n][0:prep_rows(t), :, :].rearrange("p a c -> p (a c)")
            return flat[:, 0:k * LAYER].rearrange("p (t o) -> p t o", o=LAYER)

        def slots_of(i, odd):
            slots = [(layer, where(layer, i, odd), i - layer) for layer in range(3)]
            if odd is None:
                before = [(layer, where(layer, i - 1, None), i - 1 - layer) for layer in range(3)]
                before = ([x for x in before if x[1]] or [None])[-1]
            else:
                at = slots[0][1]
                before = (2, Place(at.group - GROUPS, (at.ring - GROUPS) % 6, at.slot - 1, 1 - at.parity), i - 3)
            l0, l1, l2 = (x if x[1] else None for x in slots)
            return before, l0, l1, l2

        def prep_rows(t):
            return OPERAND_ROWS[0] if t < TILES0 else OPERAND_ROWS[1]

        def above_zero(engine, semaphore, value):
            if not isinstance(value, int) or value > 0:
                engine.wait_ge(semaphore, value)

        def iterations(engine, step):
            for i in range(4):
                step(i, None)
            with engine.Fori(2, blocks // 2) as pair:
                step(pair * 2, 0)
                step(pair * 2 + 1, 1)
            step(blocks, None)
            step(blocks + 1, None)

        def where(layer, i, odd):
            if odd is None:
                return place(layer, i - layer) if 0 <= i - layer < blocks else None
            return place(layer, i - layer, (odd + layer) % 2)

        def group_tiles(layer, q):
            return TILES0 - GROUP if (layer, q) == (0, 1) else GROUP

        block = ctx.enter_context(nc.Block())

        @block.sync
        def _(sp):
            def load_pairs(b):
                sp.dma_start(x_pairs[0:PAIRS0, 0, :],
                             x_rows[b, 0:FIELDS, :].unsqueeze(0).to_broadcast([SHIFTS, FIELDS, COLS])).then_inc(pairs_loaded, 16)
                for j in range(SHIFTS):
                    rows = x_rows[b, j:j + FIELDS, :]
                    shifted = bass.AP(tensor=rows.tensor, offset=rows.offset,
                                      ap=[[COLS, FIELDS], [SHIFTS * COLS, TILES0], [1, COLS]])
                    sp.dma_start(x_pairs[j * FIELDS:(j + 1) * FIELDS, 1:1 + TILES0, :], shifted).then_inc(pairs_loaded, 16)

            sp.dma_start(ids_all[:, :, :], ids.rearrange("(c p) f -> p c f", p=CHUNK)).then_inc(ids_loaded, 16)
            for n in range(2):
                t, k, _ = prep[n]
                sp.dma_start(swapped(n), w0b[:, t:t + k, :]).then_inc(swapped_loaded[n], 16)
            for dst, src in ((ident[:, :], ident_in), (sum32[:, :], sum32_in), (dense_sb[:, :], dense_t),
                             (wt1d_sb[:, :], wt1d), (wt3_sb[:, :], wt3), (bt1_sb[:, :], bt1), (bt2_sb[:, :], bt2)):
                sp.dma_start(dst, src).then_inc(consts_loaded, 16)

            def store(b, row, fields, done):
                sp.dma_start(x_rows[b, row:row + fields.stop - fields.start, :].rearrange("m (s d) -> s m d", d=DIM),
                             gathered[b * BLOCK:(b + 1) * BLOCK, fields, :]).then_inc(done, 16)

            early = ROWS_X - FIELDS
            sp.wait_ge(early_gathered, 16 * early)
            for b in range(PER_CHUNK):
                store(b, 0, slice(0, early), early_stored)
                store(b, FIELDS, slice(0, early), early_stored)
            sp.wait_ge(x_gathered, 16 * (FIELDS - early))
            for b in range(PER_CHUNK):
                store(b, early, slice(early, FIELDS), first_stored if b else block0_stored)
                if b == 4:
                    sp.wait_ge(early_stored, 16 * 2 * PER_CHUNK)
                    sp.wait_ge(block0_stored, 16)
                    sp.wait_ge(ones_set, 1)
                    load_pairs(0)
            sp.wait_ge(first_stored, 16 * (PER_CHUNK - 1))
            sp.wait_ge(ones_set, 3)

            def load_x_rep(b, parity, half):
                for g in range(half * GROUP, (half + 1) * GROUP):
                    fields = x_rows[b, g * FLD_IN:(g + 1) * FLD_IN, :]
                    sp.dma_start(x_rep[0:PAIRS, parity, g, :],
                                 fields.unsqueeze(0).to_broadcast([HID_IN, FLD_IN, COLS])).then_inc(x_rep_loaded[parity][half], 16)

            def load_hid(n):
                for g in range(HID_OUT):
                    maps = hid[n][g * HID_IN:(g + 1) * HID_IN, :]
                    sp.dma_start(hid_rep[n][0:PAIRS, g, :],
                                 maps.unsqueeze(1).to_broadcast([HID_IN, FLD_IN, COLS])).then_inc(hid_loaded[n], 16)

            def step(i, odd):
                l0, l1, l2 = (where(layer, i, odd) for layer in range(3))
                whole = odd is not None
                if whole or i + 1 < blocks:
                    sp.wait_ge(products_made, l0.group + GROUPS0)
                    sp.wait_ge(chunks_stored, (i + 1) // PER_CHUNK + 1)
                    load_pairs(i + 1)
                if not whole and i < blocks and l2 is None:
                    for half in range(FLD_HALVES):
                        load_x_rep(i, i % 2, half)
                if whole or i < blocks:
                    if l1 is not None:
                        sp.wait_ge(products_made, l1.group + GROUPS)
                    sp.wait_ge(hid_copied[0], i + 1)
                    load_hid(0)
                    parity = i % 2 if odd is None else odd
                    for half in range(FLD_HALVES) if l2 is not None else ():
                        sp.wait_ge(products_made, l2.group + (half + 1) * HID_OUT)
                        load_x_rep(i, parity, half)
                if l1 is not None:
                    if l2 is not None:
                        sp.wait_ge(products_made, l2.group + GROUPS)
                    sp.wait_ge(hid_copied[1], i)
                    load_hid(1)

            for i in range(4):
                step(i, None)
            with sp.Fori(2, blocks // 2 - 1) as pair:
                step(pair * 2, 0)
                step(pair * 2 + 1, 1)
            step(blocks - 2, None)
            step(blocks - 1, None)
            sp.wait_ge(products_made, place(0, blocks - 1).group + GROUPS0)
            sp.dma_start(wt1z_sb, wt1z).then_inc(top_loaded, 16)
            step(blocks, None)
            sp.wait_ge(products_made, place(1, blocks - 1).group + GROUPS)
            sp.dma_start(wt2_sb, wt2).then_inc(top2_loaded, 16)
            sp.wait_ge(y_copied, 1)
            sp.dma_start(out.rearrange("b o -> o b"), y_row).then_inc(out_stored, 16)
            sp.wait_ge(out_stored, 16)

        @block.gpsimd
        def _(pool):
            def gather(f, ids_of_field, done=x_gathered):
                pool.indirect_dma_start(gathered[:, f, :], None, tables[f],
                                        bass.IndirectOffsetOnAxis(ids_of_field, 0)).then_inc(done, 16)

            def add(s):
                pool.wait_ge(acc_copied, s + 1)
                above_zero(pool, waits_taken, s)
                pool.tensor_tensor(wait_taker[:, 1:2], wait_taker[:, 0:1], wait_taker[:, 0:1], ALU.add).then_inc(waits_taken, 1)
                pool.dma_start(acc_copy[:, :, 0:LAYER], acc_copy[:, :, LAYER:2 * LAYER],
                               accum_op=ALU.add).then_inc(y_summed, 16)

            pool.memset(wait_taker[:, :], 0.0).then_inc(taker_set, 1)
            pool.wait_ge(taker_set, 1)
            pool.wait_ge(ids_loaded, 16)
            for f in range(FIELDS):
                gather(f, ids_all[:, 0, f:f + 1], early_gathered if f < ROWS_X - FIELDS else x_gathered)
            pool.wait_ge(early_stored, 16 * 2 * PER_CHUNK)
            pool.wait_ge(block0_stored, 16)
            pool.wait_ge(first_stored, 16 * (PER_CHUNK - 1))
            pool.tensor_tensor(wait_taker[:, 2:3], wait_taker[:, 0:1], wait_taker[:, 0:1], ALU.add).then_inc(chunks_stored, 1)
            adds = FIELDS // 2 + PER_CHUNK
            done = 1 + (chunks - 1) * adds
            add(0)
            if chunks > 1:
                with pool.Fori(1, chunks) as c:
                    first = 1 + (c - 1) * adds
                    pool.tensor_copy(ids_now[:, :], ids_all[:, bass.ds(c, 1), :].rearrange("p c f -> p (c f)")).then_inc(ids_copied, 1)
                    pool.wait_ge(ids_copied, c)
                    for k in range(FIELDS // 2):
                        add(first + k)
                        gather(2 * k, ids_now[:, 2 * k:2 * k + 1])
                        gather(2 * k + 1, ids_now[:, 2 * k + 1:2 * k + 2])
                    pool.wait_ge(x_gathered, c * (16 * FIELDS) + 16 * (2 * FIELDS - ROWS_X))
                    for b in range(PER_CHUNK):
                        add(first + FIELDS // 2 + b)
                        for field, rows in ((0, FIELDS), (FIELDS, ROWS_X - FIELDS)):
                            pool.dma_start(x_rows[c * PER_CHUNK + b, field:field + rows, :].rearrange("m (s d) -> s m d", d=DIM),
                                           gathered[b * BLOCK:(b + 1) * BLOCK, 0:rows, :]).then_inc(x_stored, 16)
                    pool.wait_ge(x_stored, c * STORED)
                    pool.wait_ge(chunks_stored, c)
                    pool.tensor_tensor(wait_taker[:, 2:3], wait_taker[:, 0:1], wait_taker[:, 0:1], ALU.add).then_inc(chunks_stored, 1)
            with pool.Fori(done, total_slots) as s:
                add(s)

        @block.scalar
        def _(act):
            def load_weights(n):
                if n >= PRODUCT_RING:
                    act.wait_ge(weight_tails, n - PRODUCT_RING + 1)
                act.dma_start(staging(n), prep[n][2]).then_inc(prep_loaded[n % PRODUCT_RING], 16)

            load_weights(0)
            load_weights(1)
            for n, (t, k, _) in enumerate(prep):
                if n + 2 < len(prep):
                    load_weights(n + 2)
                if n < 2:
                    act.wait_ge(prep_added, n + 1)
                else:
                    act.wait_ge(prep_loaded[n % PRODUCT_RING], 16 * (n // PRODUCT_RING + 1))
                act.activation(weights[0:prep_rows(t), t:t + k, 0:LAYER], staging(n), ACT.Copy).then_inc(weight_heads, 1)

            def make_heads(layer, at, b, q):
                g, ring = at.group + q, (at.ring + q) % 6
                tiles = group_tiles(layer, q)
                act.wait_ge(products_made, g + 1)
                above_zero(act, groups_used, g - (SPLIT_RING - 1))
                rows = OPERAND_ROWS[layer]
                act.activation(heads[0:rows, ring % SPLIT_RING, 0:tiles, :], product[0:rows, ring % PRODUCT_RING, 0:tiles, :],
                               ACT.Copy).then_inc(heads_made, 1)

            def copy_acc(layer, at, b):
                act.wait_ge(groups_used, at.group + (GROUPS, GROUPS0)[layer == 0])
                above_zero(act, y_relued, at.slot)
                act.activation(acc_copy[:, :, :], acc[:, at.parity, :, 0:2 * LAYER], ACT.Copy).then_inc(acc_copied, 1)

            def relu(layer, at, b):
                act.wait_ge(y_summed, (at.slot + 1) * 16)
                above_zero(act, y_turned, at.slot)
                act.activation(y_relu[:, :, :], acc_copy[:, :, 0:LAYER], ACT.Relu).then_inc(y_relued, 1)

            def copy_turned(layer, at, b):
                act.wait_ge(y_turned, at.slot + 1)
                cols = slice(b * BLOCK, (b + 1) * BLOCK) if isinstance(b, int) else bass.ds(b * BLOCK, BLOCK)
                if layer < 2:
                    above_zero(act, hid_loaded[layer], b * (16 * HID_OUT))
                    act.activation(hid[layer][:, :], hid_ps[0:HALF, layer, 0:COLS], ACT.Copy).then_inc(hid_copied[layer], 1)
                    act.activation(z_t[:, layer, cols], z_ps[0:HALF, at.parity, 0:BLOCK], ACT.Copy).then_inc(z_copied, 1)
                else:
                    act.activation(z_t[:, 2:4, cols],
                                   z_ps[0:HALF, at.parity, 0:2 * BLOCK].rearrange("p (q b) -> p q b", q=2),
                                   ACT.Copy).then_inc(z_copied, 1)

            def step(i, odd):
                before, l0, l1, l2 = slots_of(i, odd)
                first, second = (l1, l2) if l1 else (l2, None)
                if before and before[0] == 0:
                    copy_acc(*before)
                    make_heads(*l0, 0)
                    relu(*before)
                    make_heads(*l0, 1)
                    copy_turned(*before)
                    before = None
                elif l0:
                    make_heads(*l0, 0)
                    make_heads(*l0, 1)
                if before:
                    copy_acc(*before)
                for q in range(2) if first else ():
                    make_heads(*first, q)
                if before:
                    relu(*before)
                if l0 and first:
                    copy_acc(*l0)
                for q in range(2, 4) if first else ():
                    make_heads(*first, q)
                if before:
                    copy_turned(*before)
                if l0 and first:
                    relu(*l0)
                for q in range(4, 6) if first else ():
                    make_heads(*first, q)
                if l0 and first:
                    copy_turned(*l0)
                for q in range(6, GROUPS) if first else ():
                    make_heads(*first, q)
                if second:
                    make_heads(*second, 0)
                    make_heads(*second, 1)
                    copy_acc(*first)
                    make_heads(*second, 2)
                    make_heads(*second, 3)
                    relu(*first)
                    make_heads(*second, 4)
                    make_heads(*second, 5)
                    copy_turned(*first)
                    make_heads(*second, 6)
                    make_heads(*second, 7)

            iterations(act, step)
            step(blocks + 2, None)

            act.wait_ge(consts_loaded, 16 * 7)
            act.wait_ge(tails_made, total_groups)
            for t in range(TOP1 // 128):
                act.wait_ge(top1_done, t + 1)
                act.activation(top1_act[:, t, :], acc[:, t // CG, t % CG, 0:batch], ACT.Relu,
                               bias=bt1_sb[:, t:t + 1]).then_inc(top1_relued, 1)
            for t in range(TOP2 // 128):
                act.wait_ge(top2_done, t + 1)
                act.activation(top2_act[:, t, :], hid_ps[:, t, 0:batch], ACT.Relu,
                               bias=bt2_sb[:, t:t + 1]).then_inc(top2_relued, 1)
            act.wait_ge(y_done, 1)
            act.activation(y_row, z_ps[0:1, 0, 0:batch], ACT.Copy).then_inc(y_copied, 1)

        @block.vector
        def _(dve):
            dve.memset(x_pairs[:, :, :], 1.0).then_inc(ones_set, 1)
            for n, (t, k, _) in enumerate(prep):
                raw = staging(n)
                if n < 2:
                    dve.wait_ge(prep_loaded[n], 16)
                    dve.wait_ge(swapped_loaded[n], 16)
                    dve.tensor_tensor(raw, raw, swapped(n), ALU.add).then_inc(prep_added, 1)
                if n == 2:
                    dve.memset(x_rep[:, :, :, :], 1.0).then_inc(ones_set, 1)
                    dve.wait_ge(prep_added, 2)
                    dve.memset(hid_rep[0][:, :, :], 1.0)
                    dve.memset(hid_rep[1][:, :, :], 1.0).then_inc(ones_set, 1)
                dve.wait_ge(weight_heads, n + 1)
                dve.tensor_tensor(weights[0:prep_rows(t), t:t + k, LAYER:2 * LAYER], raw,
                                  weights[0:prep_rows(t), t:t + k, 0:LAYER].bitcast(F32), ALU.subtract).then_inc(weight_tails, 1)

            def make_product(layer, at, q, b, parity):
                g, ring = at.group + q, (at.ring + q) % 6
                tiles, rows = group_tiles(layer, q), OPERAND_ROWS[layer]
                if layer == 0:
                    if q == 0:
                        dve.wait_ge(pairs_loaded, (b + 1) * (16 * PAIR_DMAS))
                    first, second = x_pairs[0:rows, 0, :], x_pairs[0:rows, 1 + GROUP * q:1 + GROUP * q + tiles, :]
                else:
                    half, hid_block = q // HID_OUT, q % HID_OUT
                    if q == 0:
                        dve.wait_ge(hid_loaded[layer - 1], (b + 1) * (16 * HID_OUT))
                    if hid_block == 0 and layer == 1:
                        if isinstance(b, int):
                            dve.wait_ge(x_rep_loaded[parity][half], (b // 2 + 1) * (16 * GROUP))
                        else:
                            dve.wait_ge(x_rep_loaded[parity][half], (b - parity + 2) * (8 * GROUP))
                    first = hid_rep[layer - 1][0:rows, hid_block, :]
                    second = x_rep[0:rows, parity, half * GROUP:(half + 1) * GROUP, :]
                above_zero(dve, tails_made, g - (PRODUCT_RING - 1))
                dve.tensor_tensor(product[0:rows, ring % PRODUCT_RING, 0:tiles, :],
                                  first.unsqueeze(1).to_broadcast([rows, tiles, COLS]), second,
                                  ALU.mult).then_inc(products_made, 1)

            def make_tails(layer, q, g, ring):
                tiles, rows = group_tiles(layer, q), OPERAND_ROWS[layer]
                dve.wait_ge(heads_made, g + 1)
                above_zero(dve, groups_used, g - (SPLIT_RING - 1))
                dve.tensor_tensor(tails[0:rows, ring % SPLIT_RING, 0:tiles, :],
                                  product[0:rows, ring % PRODUCT_RING, 0:tiles, :],
                                  heads[0:rows, ring % SPLIT_RING, 0:tiles, :].bitcast(F32),
                                  ALU.subtract).then_inc(tails_made, 1)

            previous = [None]

            def step(i, odd):
                for layer in range(3):
                    at = where(layer, i, odd)
                    if at is None:
                        continue
                    parity = (i - layer) % 2 if odd is None else (odd + layer) % 2
                    if odd is None and i == 1:
                        make_tails(*previous[0], at.group - 1, (at.ring - 1) % 6)
                        previous[0] = None
                    for q in range((GROUPS, GROUPS0)[layer == 0]):
                        make_product(layer, at, q, i - layer, parity)
                        if previous[0]:
                            make_tails(*previous[0], at.group + q - 1, (at.ring + q - 1) % 6)
                        previous[0] = (layer, q)

            dve.wait_ge(ones_set, 3)
            dve.wait_ge(weight_tails, len(prep))
            iterations(dve, step)
            make_tails(*previous[0], total_groups - 1, (total_groups - 1) % 6)

        @block.tensor
        def _(pe):
            pe.wait_ge(consts_loaded, 16 * 7)

            def accumulate(layer, at, b, q):
                g, ring = at.group + q, (at.ring + q) % 6
                rows, last_q = OPERAND_ROWS[layer], (GROUPS, GROUPS0)[layer == 0] - 1
                if q == 0 and isinstance(b, int) and b == 0:
                    pe.wait_ge(weight_tails, split_until[layer])
                if q == 0:
                    above_zero(pe, acc_copied, at.slot - 1)
                pe.wait_ge(tails_made, g + 1)
                tiles = group_tiles(layer, q)
                for k in range(tiles):
                    w = weights[0:rows, TILE_BASE[layer] + GROUP * q + k, :]
                    for c in range(CG):
                        cols = slice(c * 128, (c + 1) * 128)
                        nc.tensor.matmul(acc[:, at.parity, c, 0:2 * LAYER], heads[0:rows, ring % SPLIT_RING, k, cols], w,
                                         start=(q == 0 and k == 0), stop=False)
                        last = nc.tensor.matmul(acc[:, at.parity, c, LAYER:2 * LAYER], tails[0:rows, ring % SPLIT_RING, k, cols],
                                                w[:, 0:LAYER], start=False, stop=(q == last_q and k == tiles - 1))
                last.then_inc(groups_used, 1)

            def turn(layer, at, b):
                pe.wait_ge(y_relued, at.slot + 1)
                above_zero(pe, z_copied, at.slot - 1)
                if layer < 2:
                    above_zero(pe, hid_copied[layer], b)
                    for c in range(CG):
                        nc.tensor.transpose(hid_ps[0:HALF, layer, c * 128:(c + 1) * 128], y_relu[:, c, 0:HALF], ident[:, :])
                for n, first in enumerate((HALF,) if layer < 2 else (0, HALF)):
                    for c in range(CG):
                        at_col = n * BLOCK + c * (BLOCK // CG)
                        last = nc.tensor.matmul(z_ps[0:HALF, at.parity, at_col:at_col + BLOCK // CG],
                                                y_relu[:, c, first:first + HALF], sum32[:, :], start=True, stop=True)
                last.then_inc(y_turned, 1)

            def step(i, odd):
                before, l0, l1, l2 = slots_of(i, odd)
                first, second = (l1, l2) if l1 else (l2, None)
                if l0:
                    accumulate(*l0, 0)
                    if before and before[0] == 0:
                        turn(*before)
                        before = None
                    accumulate(*l0, 1)
                if first:
                    accumulate(*first, 0)
                if before:
                    turn(*before)
                for q in range(1, 3) if first else ():
                    accumulate(*first, q)
                if l0 and first:
                    turn(*l0)
                for q in range(3, GROUPS) if first else ():
                    accumulate(*first, q)
                if second:
                    for q in range(3):
                        accumulate(*second, q)
                    turn(*first)
                    for q in range(3, GROUPS):
                        accumulate(*second, q)

            iterations(pe, step)

            def top1(t, parts, end=False):
                bank, cols = acc[:, t // CG, t % CG, 0:batch], slice(t * 128, (t + 1) * 128)
                if not end:
                    nc.tensor.matmul(bank, wt1d_sb[:, cols], dense_sb[:, :], start=True, stop=False)
                for q in parts:
                    last = nc.tensor.matmul(bank, wt1z_sb[:, q, cols], z_t[:, q, :],
                                            start=False, stop=(q == Q_PARTS - 1))
                if end:
                    last.then_inc(top1_done, 1)

            last_slot = place(2, blocks - 1)
            assert last_slot.parity == 1
            pe.wait_ge(top_loaded, 16)
            pe.wait_ge(acc_copied, total_slots - 1)
            pe.wait_ge(z_copied, total_slots - 1)
            for t in range(CG):
                top1(t, (0, 1))
            turn(2, last_slot, blocks - 1)
            pe.wait_ge(acc_copied, total_slots)
            for t in range(CG, 2 * CG):
                top1(t, (0, 1))
            pe.wait_ge(z_copied, total_slots)
            for t in range(2 * CG):
                top1(t, (2, 3), end=True)
            pe.wait_ge(top2_loaded, 16)
            for k in range(TOP1 // 128):
                pe.wait_ge(top1_relued, k + 1)
                for t in range(TOP2 // 128):
                    last = nc.tensor.matmul(hid_ps[:, t, 0:batch], wt2_sb[:, k, t * 128:(t + 1) * 128], top1_act[:, k, :],
                                            start=(k == 0), stop=(k == TOP1 // 128 - 1))
                    if k == TOP1 // 128 - 1:
                        last.then_inc(top2_done, 1)
            for k in range(TOP2 // 128):
                pe.wait_ge(top2_relued, k + 1)
                last = nc.tensor.matmul(z_ps[0:1, 0, 0:batch], wt3_sb[:, k:k + 1], top2_act[:, k, :],
                                        start=(k == 0), stop=(k == TOP2 // 128 - 1))
            last.then_inc(y_done, 1)


def lay_out(inputs):
    def arr(name):
        return np.asarray(inputs[name])

    shift = np.arange(SHIFTS)[:, None, None] + SHIFTS * np.arange(TILES0)[None, None, :]
    i = np.arange(FIELDS)[None, :, None]
    i, m = np.broadcast_arrays(i, (i + shift) % FIELDS)
    w = arr("L0_rec_W0").reshape(LAYER, FIELDS, FIELDS)
    w0a = np.zeros((PAIRS0 + 1, TILES0, LAYER), w.dtype)
    w0b = np.zeros((PAIRS0 + 1, TILES0, LAYER), w.dtype)
    w0a[:PAIRS0] = w[:, i, m].transpose(1, 2, 3, 0).reshape(PAIRS0, TILES0, LAYER)
    w0a[PAIRS0, 0] = arr("L0_rec_b0")
    w0b[:PAIRS0] = w[:, m, i].transpose(1, 2, 3, 0).reshape(PAIRS0, TILES0, LAYER)
    w0b[0:FIELDS, 0] = 0
    w0b[PAIRS0 - FIELDS:PAIRS0, TILES0 - 1] = 0
    packed = {"ids": arr("ids"), "w0a": w0a, "w0b": w0b}
    for n in (1, 2):
        w = arr(f"L0_rec_W{n}").reshape(LAYER, HID_OUT, HID_IN, FLD_HALVES, GROUP, FLD_IN)
        full = np.zeros((PAIRS + 1, TILES, LAYER), w.dtype)
        full[:PAIRS] = w.transpose(2, 5, 3, 1, 4, 0).reshape(PAIRS, TILES, LAYER)
        full[PAIRS, 0] = arr(f"L0_rec_b{n}")
        packed[f"w{n}"] = full
    wt1 = arr("W_top1")
    packed["dense_t"] = np.ascontiguousarray(arr("dense_ctx").T)
    packed["wt1z"] = np.ascontiguousarray(wt1[:2 * LAYER].reshape(Q_PARTS, HALF, TOP1).transpose(1, 0, 2))
    packed["wt1d"] = np.ascontiguousarray(wt1[2 * LAYER:])
    packed["wt2"] = np.ascontiguousarray(arr("W_top2").reshape(TOP1 // 128, 128, TOP2).transpose(1, 0, 2))
    packed["wt3"] = np.ascontiguousarray(arr("W_top3").reshape(TOP2 // 128, 128).T)
    packed["bt1"] = np.ascontiguousarray(arr("b_top1").reshape(TOP1 // 128, 128).T)
    packed["bt2"] = np.ascontiguousarray(arr("b_top2").reshape(TOP2 // 128, 128).T)
    packed["ident"] = np.eye(128, dtype=np.float32)
    packed["sum32"] = np.repeat(np.eye(128 // DIM, dtype=np.float32), DIM, axis=0)
    for f in range(FIELDS):
        packed[f"tbl_{f}"] = arr(f"tbl_{f}")
    return packed


def build(nc, packed, batch):
    def dram(name):
        a = packed[name]
        return nc.dram_tensor(f"in_{name}", a.shape, mybir.dt.from_np(a.dtype), kind="ExternalInput").ap()

    args = {name: dram(name) for name in packed}
    out = nc.dram_tensor("out_y", (batch, 1), F32, kind="ExternalOutput").ap()
    cin_kernel(nc, args["ids"], [args[f"tbl_{f}"] for f in range(FIELDS)], args["w0a"], args["w0b"], args["w1"],
               args["w2"], args["dense_t"], args["wt1z"], args["wt1d"], args["wt2"], args["wt3"], args["bt1"],
               args["bt2"], args["ident"], args["sum32"], out)


def kernel(**inputs):
    import concourse.bacc as bacc
    from concourse.bass_utils import run_bass_kernel_spmd

    packed = lay_out(inputs)
    nc = bacc.Bacc("TRN2", target_bir_lowering=False, num_devices=1)
    build(nc, packed, packed["ids"].shape[0])
    r = run_bass_kernel_spmd(nc, [{f"in_{name}": a for name, a in packed.items()}], core_ids=[0])
    return r.results[0]["out_y"]
```

```python
from collections import namedtuple
from contextlib import ExitStack

import numpy as np

import concourse.bass as bass
from concourse import mybir

F32 = mybir.dt.float32
F32R = mybir.dt.float32r
I32 = mybir.dt.int32
ALU = mybir.AluOpType
ACT = mybir.ActivationFunctionType

FIELDS = 40
DIM = 32
LAYER = 200
HALF = LAYER // 2
DENSE = 16
TOP1, TOP2 = 512, 256

COLS = 256
BLOCK = COLS // DIM
CG = COLS // 128

DUO = 2 * BLOCK
FLD_PART = 128 // DUO
FLD_DMA = FIELDS // FLD_PART

SHIFTS = 3
TILES0 = (FIELDS // 2 + 1) // SHIFTS
PAIRS0 = SHIFTS * FIELDS
REPEATED = -(-(SHIFTS * TILES0 - 1) // FLD_PART)
ROWS_X = FIELDS + REPEATED * FLD_PART

HID_IN, FLD_IN = 25, 5
HID_OUT, FLD_OUT = HALF // HID_IN, FIELDS // FLD_IN
PAIRS = HID_IN * FLD_IN
TILES = HID_OUT * FLD_OUT
GROUP = 4
FLD_HALVES = FLD_OUT // GROUP
GROUPS = TILES // GROUP
GROUPS0 = 2
TILE_BASE = (0, TILES0, TILES0 + TILES)
ALL_TILES = TILES0 + 2 * TILES
OPERAND_ROWS = (PAIRS0 + 1, PAIRS + 1, PAIRS + 1)

PRODUCT_RING, HEADS_RING = 6, 4
RING = 12
PREP_TILES = 5
EARLY_LOADS = 4
Q_PARTS = 4

Place = namedtuple("Place", "group ring slot parity")


def cin_kernel(nc, ids, table_starts, table, w0a, w0b, w1, w2, dense_t, wt1z, wt1d, wt2, wt3, bt1, bt2,
               ident_in, sum32_in, out):
    duos = ids.shape[1]
    batch = duos * DUO
    blocks = batch // BLOCK
    assert blocks >= 6
    last_groups = GROUPS0 + 2 * GROUPS

    def place(layer, block, odd=None):
        if odd is None:
            i = block + layer
            group = slot = 0
            for k in range(i):
                for lay, n in ((0, GROUPS0), (1, GROUPS), (2, GROUPS)):
                    if 0 <= k - lay < blocks:
                        group, slot = group + n, slot + 1
            for lay, n in ((0, GROUPS0), (1, GROUPS))[:layer]:
                if 0 <= i - lay < blocks:
                    group, slot = group + n, slot + 1
            return Place(group, group % RING, slot, slot % 2)
        at = place(layer, 4 + odd)
        return Place(block * last_groups + (at.group - (4 + odd) * last_groups), at.ring,
                     block * 3 + (at.slot - (4 + odd) * 3), at.parity)

    total_groups = blocks * last_groups
    total_slots = blocks * 3

    ctx = ExitStack()
    with ctx:
        def sb(name, shape, dt=F32):
            return ctx.enter_context(nc.sbuf_tensor(name, shape, dt))

        def ps(name, shape, dt=F32):
            return ctx.enter_context(nc.psum_tensor(name, shape, dt))

        def sem(name):
            return ctx.enter_context(nc.semaphore(name))

        x_rows = nc.dram_tensor("x_rows", [duos, ROWS_X, 2 * COLS], F32, kind="Internal").ap()

        with nc.sbuf_tensor("raw_weights", [128, ALL_TILES, 2 * LAYER], F32) as raw_weights:
            pass
        weights = sb("weights", [128, ALL_TILES, 2 * LAYER], F32R)
        x_pairs = sb("x_pairs", [128, 1 + TILES0, COLS])
        x_rep = sb("x_rep", [128, 2, FLD_OUT, COLS])
        hid_rep = [sb(f"hid_rep{n}", [128, HID_OUT, COLS]) for n in (1, 2)]
        with nc.sbuf_tensor("product", [128, PRODUCT_RING, GROUP, COLS], F32) as product:
            pass
        tails = sb("tails", [128, PRODUCT_RING, GROUP, COLS], F32R)
        heads = sb("heads", [128, HEADS_RING, GROUP, COLS], F32R)
        acc_copy = sb("acc_copy", [128, CG, 2 * LAYER])
        y_relu = sb("y_relu", [128, CG, LAYER])
        hid = [sb(f"hid{n}", [HALF, COLS]) for n in (1, 2)]
        z_t = sb("z_t", [HALF, Q_PARTS, batch])
        gathered = sb("gathered", [128, 2, FLD_DMA, DIM])
        rows_all = sb("rows_all", [128, duos, FLD_DMA], I32)
        rows_now = sb("rows_now", [128, FLD_DMA], I32)
        starts_sb = sb("starts_sb", [128, FLD_DMA], I32)
        wait_taker = sb("wait_taker", [1, 3])
        ident = sb("ident", [128, 128])
        sum32 = sb("sum32", [128, 128 // DIM])
        dense_sb = sb("dense_sb", [DENSE, batch])
        wt1d_sb = sb("wt1d_sb", [DENSE, TOP1])
        wt3_sb = sb("wt3_sb", [128, TOP2 // 128])
        bt1_sb = sb("bt1_sb", [128, TOP1 // 128])
        bt2_sb = sb("bt2_sb", [128, TOP2 // 128])
        wt1z_sb = x_pairs[0:HALF, :, :].rearrange("p a c -> p (a c)").rearrange(
            "p (q n) -> p q n", q=Q_PARTS)
        wt2_sb = hid_rep[0][:, :, :]
        top1_act = product[:, :, :, :].rearrange("p a b c -> p (a b c)")[:, 0:TOP1 // 128 * batch].rearrange(
            "p (t n) -> p t n", t=TOP1 // 128)
        top2_act = hid_rep[1][:, :, :].rearrange("p a c -> p (a c)")[:, 0:TOP2 // 128 * batch].rearrange(
            "p (t n) -> p t n", t=TOP2 // 128)
        y_row = acc_copy[0:1, :, :].rearrange("p a c -> p (a c)")[:, 0:batch]

        acc = ps("acc", [128, 2, CG, 512])
        hid_ps = ps("hid_ps", [128, 2, 512])
        z_ps = ps("z_ps", [128, 2, 512])

        ids_loaded = sem("ids_loaded")
        consts_loaded = sem("consts_loaded")
        swapped_loaded = [sem(f"swapped_loaded{n}") for n in range(2)]
        prep_added = sem("prep_added")
        weight_heads = sem("weight_heads")
        weight_tails = sem("weight_tails")
        ones_set = sem("ones_set")
        rows_ready = sem("rows_ready")
        rows_copied = sem("rows_copied")
        taker_set = sem("taker_set")
        waits_taken = sem("waits_taken")
        x_gathered = sem("x_gathered")
        first_gathered = sem("first_gathered")
        x_stored = sem("x_stored")
        first_stored = [sem("first_stored0"), sem("first_stored1")]
        duos_stored = sem("duos_stored")
        pairs_loaded = sem("pairs_loaded")
        x_rep_loaded = [[sem(f"x_rep_loaded{p}{h}") for h in range(FLD_HALVES)] for p in range(2)]
        hid_loaded = [sem("hid_loaded1"), sem("hid_loaded2")]
        products_made = sem("products_made")
        heads_made = sem("heads_made")
        tails_made = sem("tails_made")
        groups_used = sem("groups_used")
        acc_copied = sem("acc_copied")
        y_summed = sem("y_summed")
        y_relued = sem("y_relued")
        y_turned = sem("y_turned")
        z_copied = sem("z_copied")
        hid_copied = [sem("hid_copied1"), sem("hid_copied2")]
        top_loaded = sem("top_loaded")
        top2_loaded = sem("top2_loaded")
        top1_done = sem("top1_done")
        top1_relued = sem("top1_relued")
        top2_done = sem("top2_done")
        top2_relued = sem("top2_relued")
        y_done = sem("y_done")
        y_copied = sem("y_copied")
        out_stored = sem("out_stored")

        PAIR_DMAS = 1 + SHIFTS
        EARLY_DUOS = 2
        CONSTS = 7
        GATHERS, STORES = 16 * FLD_DMA, 16 * 2
        prep = [(0, GROUP, w0a[:, 0:GROUP, :]), (GROUP, TILES0 - GROUP, w0a[:, GROUP:TILES0, :])]
        for layer, w in ((1, w1), (2, w2)):
            for t in range(0, TILES, PREP_TILES):
                k = min(PREP_TILES, TILES - t)
                prep.append((TILE_BASE[layer] + t, k, w[:, t:t + k, :]))
        split_until = [2, 2 + -(-TILES // PREP_TILES), len(prep)]

        prep_loaded = [sem(f"prep_loaded{n}") for n in range(len(prep))]

        def split_after(i, layer=None, q=None):
            w1 = list(range(split_until[0], split_until[1]))
            w2 = list(range(split_until[1], split_until[2]))
            if i == "start":
                return list(range(split_until[0]))
            if (i, layer) == (0, 0):
                return w1[:4]
            if (i, layer) == (1, 0):
                return w1[4:]
            if layer == 1 and i in (1, 2):
                n = (i - 1) * (GROUPS // 2) + q // 2
                return w2[n:n + 1]
            return []

        def raw(n):
            t, k, _ = prep[n]
            return raw_weights[0:prep_rows(t), t:t + k, LAYER:2 * LAYER]

        def swapped(n):
            t, k, _ = prep[n]
            flat = hid_rep[n][0:prep_rows(t), :, :].rearrange("p a c -> p (a c)")
            return flat[:, 0:k * LAYER].rearrange("p (t o) -> p t o", o=LAYER)

        def slots_of(i, odd):
            slots = [(layer, where(layer, i, odd), i - layer) for layer in range(3)]
            if odd is None:
                before = [(layer, where(layer, i - 1, None), i - 1 - layer) for layer in range(3)]
                before = ([x for x in before if x[1]] or [None])[-1]
            else:
                at = slots[0][1]
                before = (2, Place(at.group - GROUPS, (at.ring - GROUPS) % RING, at.slot - 1, 1 - at.parity), i - 3)
            l0, l1, l2 = (x if x[1] else None for x in slots)
            return before, l0, l1, l2

        def prep_rows(t):
            return OPERAND_ROWS[0] if t < TILES0 else OPERAND_ROWS[1]

        def above_zero(engine, semaphore, value):
            if not isinstance(value, int) or value > 0:
                engine.wait_ge(semaphore, value)

        def iterations(engine, step):
            for i in range(4):
                step(i, None)
            with engine.Fori(2, blocks // 2) as pair:
                step(pair * 2, 0)
                step(pair * 2 + 1, 1)
            step(blocks, None)
            step(blocks + 1, None)

        def where(layer, i, odd):
            if odd is None:
                return place(layer, i - layer) if 0 <= i - layer < blocks else None
            return place(layer, i - layer, (odd + layer) % 2)

        def group_tiles(layer, q):
            return TILES0 - GROUP if (layer, q) == (0, 1) else GROUP

        block = ctx.enter_context(nc.Block())

        def stored_parts(duo, buffer):
            rows = x_rows[duo, 0:ROWS_X, :].rearrange("(k f) (s d) -> (f s) k d", f=FLD_PART, d=DIM)
            return ((rows[:, 0:FLD_DMA, :], gathered[:, buffer, :, :]),
                    (rows[:, FLD_DMA:FLD_DMA + REPEATED, :], gathered[:, buffer, 0:REPEATED, :]))

        @block.sync
        def _(sp):
            def block_rows(duo, parity, first, n):
                return x_rows[parity // 2:duos, :, :][duo, first:first + n, (parity % 2) * COLS:(parity % 2 + 1) * COLS]

            def load_pairs(duo, parity):
                sp.dma_start(x_pairs[0:PAIRS0, 0, :],
                             block_rows(duo, parity, 0, FIELDS).unsqueeze(0).to_broadcast([SHIFTS, FIELDS, COLS])).then_inc(pairs_loaded, 16)
                for j in range(SHIFTS):
                    rows = block_rows(duo, parity, j, FIELDS)
                    shifted = bass.AP(tensor=rows.tensor, offset=rows.offset,
                                      ap=[[2 * COLS, FIELDS], [SHIFTS * 2 * COLS, TILES0], [1, COLS]])
                    sp.dma_start(x_pairs[j * FIELDS:(j + 1) * FIELDS, 1:1 + TILES0, :], shifted).then_inc(pairs_loaded, 16)

            sp.dma_start(rows_all[:, :, :], ids).then_inc(ids_loaded, 16)
            sp.dma_start(starts_sb[:, :], table_starts).then_inc(ids_loaded, 16)
            for n in range(2):
                t, k, _ = prep[n]
                sp.dma_start(swapped(n), w0b[:, t:t + k, :]).then_inc(swapped_loaded[n], 16)
            for dst, src in ((ident[:, :], ident_in), (sum32[:, :], sum32_in), (dense_sb[:, :], dense_t),
                             (wt1d_sb[:, :], wt1d), (wt3_sb[:, :], wt3), (bt1_sb[:, :], bt1), (bt2_sb[:, :], bt2)):
                sp.dma_start(dst, src).then_inc(consts_loaded, 16)

            def load_x_rep(duo, parity, half):
                early = isinstance(duo, int) and duo < EARLY_DUOS
                maps = HID_IN if early else HID_IN - 1
                for g in reversed(range(half * GROUP, (half + 1) * GROUP)):
                    fields = block_rows(duo, parity, g * FLD_IN, FLD_IN)
                    sp.dma_start(x_rep[0:maps * FLD_IN, parity, g, :],
                                 fields.unsqueeze(0).to_broadcast([maps, FLD_IN, COLS])).then_inc(x_rep_loaded[parity][half], 16)
                if not early:
                    groups = block_rows(duo, parity, half * GROUP * FLD_IN, GROUP * FLD_IN)
                    sp.dma_start(x_rep[maps * FLD_IN:PAIRS, parity, half * GROUP:(half + 1) * GROUP, :],
                                 groups.rearrange("(g f) c -> f g c", f=FLD_IN)).then_inc(x_rep_loaded[parity][half], 16)

            def store(duo):
                for part in stored_parts(duo, duo):
                    sp.dma_start(*part).then_inc(first_stored[duo], 16)

            sp.wait_ge(first_gathered, GATHERS)
            store(0)
            sp.wait_ge(first_stored[0], STORES)
            sp.wait_ge(ones_set, 1)
            load_pairs(0, 0)
            sp.wait_ge(ones_set, 2)
            for half in range(FLD_HALVES):
                load_x_rep(0, 0, half)
            sp.wait_ge(x_gathered, GATHERS)
            store(1)
            sp.wait_ge(ones_set, 3)

            def load_hid(n):
                for g in range(HID_OUT):
                    maps = hid[n][g * HID_IN:(g + 1) * HID_IN, :]
                    sp.dma_start(hid_rep[n][0:PAIRS, g, :],
                                 maps.unsqueeze(1).to_broadcast([HID_IN, FLD_IN, COLS])).then_inc(hid_loaded[n], 16)

            def step(i, odd, duo=None):
                l0, l1, l2 = (where(layer, i, odd) for layer in range(3))
                whole = odd is not None
                parity = odd if whole else i % 2
                duo = duo if whole else i // 2
                if whole or i + 1 < blocks:
                    if whole:
                        sp.wait_ge(hid_copied[0], i + 1)
                    else:
                        sp.wait_ge(products_made, l0.group + GROUPS0)
                    if parity and (whole or i > 2):
                        sp.wait_ge(duos_stored, duo)
                    elif parity:
                        sp.wait_ge(first_stored[1], STORES)
                    load_pairs(duo, 1 + parity)
                if not whole and 0 < i < blocks and l2 is None:
                    for half in range(FLD_HALVES):
                        load_x_rep(duo, parity, half)
                if whole or i < blocks:
                    if not whole:
                        sp.wait_ge(hid_copied[0], i + 1)
                    if l1 is not None:
                        sp.wait_ge(products_made, l1.group + GROUPS)
                    load_hid(0)
                    for half in range(FLD_HALVES) if l2 is not None else ():
                        sp.wait_ge(products_made, l2.group + (half + 1) * HID_OUT)
                        load_x_rep(duo, parity, half)
                if l1 is not None:
                    sp.wait_ge(hid_copied[1], i)
                    if l2 is not None:
                        sp.wait_ge(products_made, l2.group + GROUPS)
                    load_hid(1)

            for i in range(4):
                step(i, None)
            with sp.Fori(2, duos - 1) as duo:
                step(duo * 2, 0, duo)
                step(duo * 2 + 1, 1, duo)
            step(blocks - 2, None)
            step(blocks - 1, None)
            sp.wait_ge(products_made, place(0, blocks - 1).group + GROUPS0)
            sp.dma_start(wt1z_sb, wt1z).then_inc(top_loaded, 16)
            step(blocks, None)
            sp.wait_ge(products_made, place(1, blocks - 1).group + GROUPS)
            sp.dma_start(wt2_sb, wt2).then_inc(top2_loaded, 16)
            sp.wait_ge(y_copied, 1)
            sp.dma_start(out.rearrange("b o -> o b"), y_row).then_inc(out_stored, 16)
            sp.wait_ge(out_stored, 16)

        @block.gpsimd
        def _(pool):
            def gather(buffer, k, rows, done):
                pool.indirect_dma_start(gathered[:, buffer, k, :], None, table,
                                        bass.IndirectOffsetOnAxis(rows, 0)).then_inc(done, 16)

            def add(s):
                pool.wait_ge(acc_copied, s + 1)
                above_zero(pool, waits_taken, s)
                pool.tensor_tensor(wait_taker[:, 1:2], wait_taker[:, 0:1], wait_taker[:, 0:1], ALU.add).then_inc(waits_taken, 1)
                pool.dma_start(acc_copy[:, :, 0:LAYER], acc_copy[:, :, LAYER:2 * LAYER],
                               accum_op=ALU.add).then_inc(y_summed, 16)

            pool.memset(wait_taker[:, :], 0.0).then_inc(taker_set, 1)
            pool.wait_ge(taker_set, 1)
            pool.wait_ge(rows_ready, 1)
            for duo, gathers_done in ((0, first_gathered), (1, x_gathered)):
                for k in range(FLD_DMA):
                    gather(duo, k, rows_all[:, duo, k:k + 1], gathers_done)
            pool.wait_ge(first_stored[0], STORES)
            add(0)
            adds = 6
            assert adds > FLD_DMA
            with pool.Fori(2, duos) as duo:
                first = 1 + (duo - 2) * adds
                pool.tensor_copy(rows_now[:, :], rows_all[:, bass.ds(duo, 1), :].rearrange("p c k -> p (c k)")).then_inc(rows_copied, 1)
                pool.wait_ge(rows_copied, duo - 1)
                for k in range(FLD_DMA):
                    add(first + k)
                    gather(0, k, rows_now[:, k:k + 1], x_gathered)
                pool.wait_ge(x_gathered, duo * GATHERS)
                add(first + FLD_DMA)
                for part in stored_parts(duo, 0):
                    pool.dma_start(*part).then_inc(x_stored, 16)
                pool.wait_ge(x_stored, (duo - 1) * STORES)
                pool.tensor_tensor(wait_taker[:, 2:3], wait_taker[:, 0:1], wait_taker[:, 0:1], ALU.add).then_inc(duos_stored, 1)
                pool.wait_ge(duos_stored, duo - 1)
            done = 1 + (duos - 2) * adds
            with pool.Fori(done, total_slots) as s:
                add(s)

        @block.scalar
        def _(act):
            loads = [0]

            def load_weights(until):
                while loads[0] < min(until, len(prep)):
                    n = loads[0]
                    act.dma_start(raw(n), prep[n][2]).then_inc(prep_loaded[n], 16)
                    loads[0] += 1

            def split_heads(*chunks_now):
                for n in chunks_now:
                    t, k, _ = prep[n]
                    if n < 2:
                        act.wait_ge(prep_added, n + 1)
                    else:
                        act.wait_ge(prep_loaded[n], 16)
                    act.activation(weights[0:prep_rows(t), t:t + k, 0:LAYER], raw(n), ACT.Copy).then_inc(weight_heads, 1)
                    if n in split_after(0, 0) or n > split_until[1]:
                        load_weights(n + 1 + EARLY_LOADS)

            load_weights(EARLY_LOADS)
            split_heads(*split_after("start"))

            def make_heads(layer, at, b, q):
                g, ring = at.group + q, (at.ring + q) % RING
                tiles = group_tiles(layer, q)
                act.wait_ge(products_made, g + 1)
                above_zero(act, groups_used, g - (HEADS_RING - 1))
                rows = OPERAND_ROWS[layer]
                act.activation(heads[0:rows, ring % HEADS_RING, 0:tiles, :], product[0:rows, ring % PRODUCT_RING, 0:tiles, :],
                               ACT.Copy).then_inc(heads_made, 1)

            def copy_acc(layer, at, b):
                act.wait_ge(groups_used, at.group + (GROUPS, GROUPS0)[layer == 0])
                above_zero(act, y_relued, at.slot)
                act.activation(acc_copy[:, :, :], acc[:, at.parity, :, 0:2 * LAYER], ACT.Copy).then_inc(acc_copied, 1)

            def relu(layer, at, b):
                act.wait_ge(y_summed, (at.slot + 1) * 16)
                above_zero(act, y_turned, at.slot)
                act.activation(y_relu[:, :, :], acc_copy[:, :, 0:LAYER], ACT.Relu).then_inc(y_relued, 1)

            def copy_turned(layer, at, b):
                act.wait_ge(y_turned, at.slot + 1)
                cols = slice(b * BLOCK, (b + 1) * BLOCK) if isinstance(b, int) else bass.ds(b * BLOCK, BLOCK)
                if layer < 2:
                    above_zero(act, hid_loaded[layer], b * (16 * HID_OUT))
                    act.activation(hid[layer][:, :], hid_ps[0:HALF, layer, 0:COLS], ACT.Copy).then_inc(hid_copied[layer], 1)
                    act.activation(z_t[:, layer, cols], z_ps[0:HALF, at.parity, 0:BLOCK], ACT.Copy).then_inc(z_copied, 1)
                else:
                    act.activation(z_t[:, 2:4, cols],
                                   z_ps[0:HALF, at.parity, 0:2 * BLOCK].rearrange("p (q b) -> p q b", q=2),
                                   ACT.Copy).then_inc(z_copied, 1)

            def heads_and_results(slot, previous):
                make_heads(*slot, 0)
                make_heads(*slot, 1)
                copy_acc(*previous)
                make_heads(*slot, 2)
                make_heads(*slot, 3)
                relu(*previous)
                make_heads(*slot, 4)
                make_heads(*slot, 5)
                copy_turned(*previous)
                make_heads(*slot, 6)
                make_heads(*slot, 7)

            def step(i, odd):
                before, l0, l1, l2 = slots_of(i, odd)
                first, second = (l1, l2) if l1 else (l2, None)
                if first and not l0:
                    heads_and_results(first, before)
                    if second:
                        heads_and_results(second, first)
                    return
                if before and before[0] == 0:
                    copy_acc(*before)
                    make_heads(*l0, 0)
                    relu(*before)
                    make_heads(*l0, 1)
                    copy_turned(*before)
                    before = None
                    split_heads(*split_after(i, 0, 0))
                elif l0:
                    make_heads(*l0, 0)
                    make_heads(*l0, 1)
                    if odd is None and i == 0:
                        load_weights(split_until[0] + EARLY_LOADS)
                    split_heads(*(split_after(i, 0, 0) if odd is None else ()))

                def split_now(q):
                    return split_after(i, 1, q) if odd is None and l1 else ()

                if before:
                    copy_acc(*before)
                split_heads(*split_now(0))
                for q in range(2) if first else ():
                    make_heads(*first, q)
                if odd is None and i == 1:
                    load_weights(split_until[1] + 1 + EARLY_LOADS)
                if before:
                    relu(*before)
                if l0 and first:
                    copy_acc(*l0)
                split_heads(*split_now(2))
                for q in range(2, 4) if first else ():
                    make_heads(*first, q)
                if before:
                    copy_turned(*before)
                if l0 and first:
                    relu(*l0)
                split_heads(*split_now(4))
                for q in range(4, 6) if first else ():
                    make_heads(*first, q)
                if l0 and first:
                    copy_turned(*l0)
                split_heads(*split_now(6))
                for q in range(6, GROUPS) if first else ():
                    make_heads(*first, q)
                if second:
                    heads_and_results(second, first)

            iterations(act, step)
            step(blocks + 2, None)

            act.wait_ge(consts_loaded, 16 * CONSTS)
            act.wait_ge(groups_used, total_groups)
            for t in range(TOP1 // 128):
                act.wait_ge(top1_done, t + 1)
                act.activation(top1_act[:, t, :], acc[:, t // CG, t % CG, 0:batch], ACT.Relu,
                               bias=bt1_sb[:, t:t + 1]).then_inc(top1_relued, 1)
            for t in range(TOP2 // 128):
                act.wait_ge(top2_done, t + 1)
                act.activation(top2_act[:, t, :], hid_ps[:, t, 0:batch], ACT.Relu,
                               bias=bt2_sb[:, t:t + 1]).then_inc(top2_relued, 1)
            act.wait_ge(y_done, 1)
            act.activation(y_row, z_ps[0:1, 0, 0:batch], ACT.Copy).then_inc(y_copied, 1)

        @block.vector
        def _(dve):
            dve.memset(x_pairs[:, :, :], 1.0).then_inc(ones_set, 1)
            dve.wait_ge(ids_loaded, 16 * 2)
            dve.tensor_tensor(rows_all[:, :, :], rows_all[:, :, :],
                              starts_sb[:, :].unsqueeze(1).to_broadcast([128, duos, FLD_DMA]), ALU.add).then_inc(rows_ready, 1)
            dve.memset(x_rep[:, :, :, :], 1.0).then_inc(ones_set, 1)

            def split_tails(*chunks_now):
                for n in chunks_now:
                    t, k, _ = prep[n]
                    dve.wait_ge(weight_heads, n + 1)
                    dve.tensor_tensor(weights[0:prep_rows(t), t:t + k, LAYER:2 * LAYER], raw(n),
                                      weights[0:prep_rows(t), t:t + k, 0:LAYER].bitcast(F32), ALU.subtract).then_inc(weight_tails, 1)

            for n in range(2):
                dve.wait_ge(prep_loaded[n], 16)
                dve.wait_ge(swapped_loaded[n], 16)
                dve.tensor_tensor(raw(n), raw(n), swapped(n), ALU.add).then_inc(prep_added, 1)
            dve.wait_ge(prep_added, 2)
            dve.memset(hid_rep[0][:, :, :], 1.0)
            dve.memset(hid_rep[1][:, :, :], 1.0).then_inc(ones_set, 1)
            split_tails(*split_after("start"))

            def x_rep_count(b, parity):
                if isinstance(b, int) and b // 2 < EARLY_DUOS:
                    return (b // 2 + 1) * (16 * GROUP)
                return (b - parity + 2) * (8 * (GROUP + 1)) - EARLY_DUOS * 16

            def make_products(layer, at, q, b, parity):
                g, place0 = at.group + q, (at.ring + q) % PRODUCT_RING
                rows = OPERAND_ROWS[layer]
                out = product[0:rows, place0:place0 + 2, :, :]
                if layer == 0:
                    dve.wait_ge(pairs_loaded, (b + 1) * (16 * PAIR_DMAS))
                    first = x_pairs[0:rows, 0, :].unsqueeze(1).to_broadcast([rows, TILES0, COLS])
                    second = x_pairs[0:rows, 1:1 + TILES0, :]
                    out = out.rearrange("p a b c -> p (a b) c")[:, 0:TILES0, :]
                else:
                    half, hid_block = q // HID_OUT, q % HID_OUT
                    if q == 0:
                        dve.wait_ge(hid_loaded[layer - 1], (b + 1) * (16 * HID_OUT))
                    if hid_block == 0 and layer == 1:
                        dve.wait_ge(x_rep_loaded[parity][half], x_rep_count(b, parity))
                    shape = [rows, 2, GROUP, COLS]
                    first = hid_rep[layer - 1][0:rows, hid_block:hid_block + 2, :].unsqueeze(2).to_broadcast(shape)
                    second = x_rep[0:rows, parity, half * GROUP:(half + 1) * GROUP, :].unsqueeze(1).to_broadcast(shape)
                above_zero(dve, groups_used, g - (PRODUCT_RING - 2))
                dve.tensor_tensor(out, first, second, ALU.mult).then_inc(products_made, 2)

            def make_tails(layer, q, g, ring):
                tiles, rows = group_tiles(layer, q), OPERAND_ROWS[layer]
                dve.wait_ge(heads_made, g + 1)
                dve.tensor_tensor(tails[0:rows, ring % PRODUCT_RING, 0:tiles, :],
                                  product[0:rows, ring % PRODUCT_RING, 0:tiles, :],
                                  heads[0:rows, ring % HEADS_RING, 0:tiles, :].bitcast(F32),
                                  ALU.subtract).then_inc(tails_made, 1)

            previous = [None]

            def make_previous_tails(g, ring):
                layer, q = previous[0]
                for n in (2, 1):
                    make_tails(layer, q + 2 - n, g - n, (ring - n) % RING)
                previous[0] = None

            def step(i, odd):
                for layer in range(3):
                    at = where(layer, i, odd)
                    if at is None:
                        continue
                    parity = (i - layer) % 2 if odd is None else (odd + layer) % 2
                    for q in range(0, (GROUPS, GROUPS0)[layer == 0], 2):
                        make_products(layer, at, q, i - layer, parity)
                        if previous[0]:
                            make_previous_tails(at.group + q, at.ring + q)
                        previous[0] = (layer, q)
                        if odd is None and (i == 0 or i == 1 and (layer, q) in ((0, 0), (1, 0))):
                            make_previous_tails(at.group + 2, at.ring + 2)
                        if odd is None:
                            split_tails(*split_after(i, layer, q))

            dve.wait_ge(ones_set, 3)
            iterations(dve, step)
            make_previous_tails(total_groups, total_groups)

        @block.tensor
        def _(pe):
            pe.wait_ge(consts_loaded, 16 * CONSTS)

            def accumulate(layer, at, b, q):
                g, ring = at.group + q, (at.ring + q) % RING
                rows, last_q = OPERAND_ROWS[layer], (GROUPS, GROUPS0)[layer == 0] - 1
                if q == 0 and isinstance(b, int) and b == 0:
                    pe.wait_ge(weight_tails, split_until[layer])
                if q == 0:
                    above_zero(pe, acc_copied, at.slot - 1)
                pe.wait_ge(tails_made, g + 1)
                tiles = group_tiles(layer, q)
                for k in range(tiles):
                    w = weights[0:rows, TILE_BASE[layer] + GROUP * q + k, :]
                    for c in range(CG):
                        cols = slice(c * 128, (c + 1) * 128)
                        nc.tensor.matmul(acc[:, at.parity, c, 0:2 * LAYER], heads[0:rows, ring % HEADS_RING, k, cols], w,
                                         start=(q == 0 and k == 0), stop=False)
                        last = nc.tensor.matmul(acc[:, at.parity, c, LAYER:2 * LAYER], tails[0:rows, ring % PRODUCT_RING, k, cols],
                                                w[:, 0:LAYER], start=False, stop=(q == last_q and k == tiles - 1))
                last.then_inc(groups_used, 1)

            def turn(layer, at, b):
                pe.wait_ge(y_relued, at.slot + 1)
                above_zero(pe, z_copied, at.slot - 1)
                if layer < 2:
                    above_zero(pe, hid_copied[layer], b)
                    for c in range(CG):
                        nc.tensor.transpose(hid_ps[0:HALF, layer, c * 128:(c + 1) * 128], y_relu[:, c, 0:HALF], ident[:, :])
                for n, first in enumerate((HALF,) if layer < 2 else (0, HALF)):
                    for c in range(CG):
                        at_col = n * BLOCK + c * (BLOCK // CG)
                        last = nc.tensor.matmul(z_ps[0:HALF, at.parity, at_col:at_col + BLOCK // CG],
                                                y_relu[:, c, first:first + HALF], sum32[:, :], start=True, stop=True)
                last.then_inc(y_turned, 1)

            def step(i, odd):
                before, l0, l1, l2 = slots_of(i, odd)
                first, second = (l1, l2) if l1 else (l2, None)
                if before and before[0] == 0:
                    turn(*before)
                    before = None
                if l0:
                    accumulate(*l0, 0)
                    accumulate(*l0, 1)
                if l0 and first:
                    accumulate(*first, 0)
                if l0 and before:
                    turn(*before)
                for q in range(1 if l0 else 0, 3) if first else ():
                    accumulate(*first, q)
                if before and not l0:
                    turn(*before)
                if l0 and first:
                    turn(*l0)
                for q in range(3, GROUPS) if first else ():
                    accumulate(*first, q)
                if second:
                    for q in range(3):
                        accumulate(*second, q)
                    turn(*first)
                    for q in range(3, GROUPS):
                        accumulate(*second, q)

            iterations(pe, step)

            def top1(t, parts, end=False):
                bank, cols = acc[:, t // CG, t % CG, 0:batch], slice(t * 128, (t + 1) * 128)
                if not end:
                    nc.tensor.matmul(bank, wt1d_sb[:, cols], dense_sb[:, :], start=True, stop=False)
                for q in parts:
                    last = nc.tensor.matmul(bank, wt1z_sb[:, q, cols], z_t[:, q, :],
                                            start=False, stop=(q == Q_PARTS - 1))
                if end:
                    last.then_inc(top1_done, 1)

            last_slot = place(2, blocks - 1)
            assert last_slot.parity == 1
            pe.wait_ge(top_loaded, 16)
            pe.wait_ge(acc_copied, total_slots - 1)
            pe.wait_ge(z_copied, total_slots - 1)
            for t in range(CG):
                top1(t, (0, 1))
            turn(2, last_slot, blocks - 1)
            pe.wait_ge(acc_copied, total_slots)
            for t in range(CG, 2 * CG):
                top1(t, (0, 1))
            pe.wait_ge(z_copied, total_slots)
            for t in range(2 * CG):
                top1(t, (2, 3), end=True)
            pe.wait_ge(top2_loaded, 16)
            for k in range(TOP1 // 128):
                pe.wait_ge(top1_relued, k + 1)
                for t in range(TOP2 // 128):
                    last = nc.tensor.matmul(hid_ps[:, t, 0:batch], wt2_sb[:, k, t * 128:(t + 1) * 128], top1_act[:, k, :],
                                            start=(k == 0), stop=(k == TOP1 // 128 - 1))
                    if k == TOP1 // 128 - 1:
                        last.then_inc(top2_done, 1)
            for k in range(TOP2 // 128):
                pe.wait_ge(top2_relued, k + 1)
                last = nc.tensor.matmul(z_ps[0:1, 0, 0:batch], wt3_sb[:, k:k + 1], top2_act[:, k, :],
                                        start=(k == 0), stop=(k == TOP2 // 128 - 1))
            last.then_inc(y_done, 1)


def lay_out(inputs):
    def arr(name):
        return np.asarray(inputs[name])

    shift = np.arange(SHIFTS)[:, None, None] + SHIFTS * np.arange(TILES0)[None, None, :]
    i = np.arange(FIELDS)[None, :, None]
    i, m = np.broadcast_arrays(i, (i + shift) % FIELDS)
    w = arr("L0_rec_W0").reshape(LAYER, FIELDS, FIELDS)
    w0a = np.zeros((PAIRS0 + 1, TILES0, LAYER), w.dtype)
    w0b = np.zeros((PAIRS0 + 1, TILES0, LAYER), w.dtype)
    w0a[:PAIRS0] = w[:, i, m].transpose(1, 2, 3, 0).reshape(PAIRS0, TILES0, LAYER)
    w0a[PAIRS0, 0] = arr("L0_rec_b0")
    w0b[:PAIRS0] = w[:, m, i].transpose(1, 2, 3, 0).reshape(PAIRS0, TILES0, LAYER)
    w0b[0:FIELDS, 0] = 0
    w0b[PAIRS0 - FIELDS:PAIRS0, TILES0 - 1] = 0
    batch = arr("ids").shape[0]
    ids = arr("ids").reshape(batch // DUO, DUO, FLD_DMA, FLD_PART).transpose(3, 1, 0, 2)
    packed = {"ids": np.ascontiguousarray(ids.reshape(128, batch // DUO, FLD_DMA)), "w0a": w0a, "w0b": w0b}
    for n in (1, 2):
        w = arr(f"L0_rec_W{n}").reshape(LAYER, HID_OUT, HID_IN, FLD_HALVES, GROUP, FLD_IN)
        full = np.zeros((PAIRS + 1, TILES, LAYER), w.dtype)
        full[:PAIRS] = w.transpose(2, 5, 3, 1, 4, 0).reshape(PAIRS, TILES, LAYER)
        full[PAIRS, 0] = arr(f"L0_rec_b{n}")
        packed[f"w{n}"] = full
    wt1 = arr("W_top1")
    packed["dense_t"] = np.ascontiguousarray(arr("dense_ctx").T)
    packed["wt1z"] = np.ascontiguousarray(wt1[:2 * LAYER].reshape(Q_PARTS, HALF, TOP1).transpose(1, 0, 2))
    packed["wt1d"] = np.ascontiguousarray(wt1[2 * LAYER:])
    packed["wt2"] = np.ascontiguousarray(arr("W_top2").reshape(TOP1 // 128, 128, TOP2).transpose(1, 0, 2))
    packed["wt3"] = np.ascontiguousarray(arr("W_top3").reshape(TOP2 // 128, 128).T)
    packed["bt1"] = np.ascontiguousarray(arr("b_top1").reshape(TOP1 // 128, 128).T)
    packed["bt2"] = np.ascontiguousarray(arr("b_top2").reshape(TOP2 // 128, 128).T)
    packed["ident"] = np.eye(128, dtype=np.float32)
    packed["sum32"] = np.repeat(np.eye(128 // DIM, dtype=np.float32), DIM, axis=0)
    tables = [arr(f"tbl_{f}") for f in range(FIELDS)]
    packed["table"] = np.concatenate(tables)
    starts = np.cumsum([0] + [t.shape[0] for t in tables[:-1]]).astype(np.int32)
    packed["table_starts"] = np.repeat(starts.reshape(FLD_DMA, FLD_PART).T, DUO, axis=0)
    return packed


def build(nc, packed, batch):
    def dram(name):
        a = packed[name]
        return nc.dram_tensor(f"in_{name}", a.shape, mybir.dt.from_np(a.dtype), kind="ExternalInput").ap()

    args = {name: dram(name) for name in packed}
    out = nc.dram_tensor("out_y", (batch, 1), F32, kind="ExternalOutput").ap()
    cin_kernel(nc, args["ids"], args["table_starts"], args["table"], args["w0a"], args["w0b"], args["w1"],
               args["w2"], args["dense_t"], args["wt1z"], args["wt1d"], args["wt2"], args["wt3"], args["bt1"],
               args["bt2"], args["ident"], args["sum32"], out)


def kernel(**inputs):
    import concourse.bacc as bacc
    from concourse.bass_utils import run_bass_kernel_spmd

    packed = lay_out(inputs)
    nc = bacc.Bacc("TRN2", target_bir_lowering=False, num_devices=1)
    build(nc, packed, packed["dense_t"].shape[1])
    r = run_bass_kernel_spmd(nc, [{f"in_{name}": a for name, a in packed.items()}], core_ids=[0])
    return r.results[0]["out_y"]
```
